# Optimizing a Trainium2 kernel written in Bass

```python
import numpy as np
import jax
import jax.numpy as jnp

def _softmax(x, axis=-1):
    return jax.nn.softmax(x, axis=axis)

def _gelu(x):
    return jax.nn.gelu(x, approximate=True)

def _silu(x):
    return jax.nn.silu(x)

def _sigmoid(x):
    return jax.nn.sigmoid(x)

def _layernorm(x, axis=-1, eps=1e-05):
    m = jnp.mean(x, axis=axis, keepdims=True)
    v = jnp.var(x, axis=axis, keepdims=True)
    return (x - m) / jnp.sqrt(v + eps)

def _scatter_add(tgt, idx, src, axis=0):
    return tgt.at[idx].add(src)

def _segment_sum(src, seg, n):
    return jax.ops.segment_sum(src, seg, n)
kernel_name = 'mk_adaln_d1_jaxref_r4_3edea1'

def setup_inputs(seed: int=0):
    np.random.seed(seed)
    _w = jnp.asarray

    def _L0_attn_setup():
        import jax, jax.numpy as jnp
        import numpy as np
        N_HEAD = 16
        W_SCALE = 0.02
        key = jax.random.key(seed)
        ks = jax.random.split(key, 9)
        B, T, C = (4, 512, 256)
        x = jax.random.normal(ks[0], (B, T, C), dtype=jnp.float32)

        def w(k):
            return jax.random.normal(k, (C, C), dtype=jnp.float32) * W_SCALE
        return {'x': x, 'Wq': w(ks[1]), 'bq': jnp.zeros((C,), jnp.float32), 'Wk': w(ks[2]), 'bk': jnp.zeros((C,), jnp.float32), 'Wv': w(ks[3]), 'bv': jnp.zeros((C,), jnp.float32), 'Wp': w(ks[4]), 'bp': jnp.zeros((C,), jnp.float32)}
    _L0_attn_in = _L0_attn_setup()

    def _L0_ffn_setup():
        import jax, jax.numpy as jnp
        import numpy as np
        DIM = 256
        DEPTH = 2
        HEADS = 8
        DIM_HEAD = 64
        WINDOW = 128
        INNER = HEADS * DIM_HEAD
        HID = int(DIM * 4 * 2 / 3)
        B, N = (2, 2048)
        QK_SCALE = 8.0

        def shift_token(t):
            t1, t2 = jnp.split(t, 2, axis=-1)
            t2 = jnp.pad(t2, ((0, 0), (1, 0), (0, 0)))[:, :-1]
            return jnp.concatenate([t1, t2], axis=-1)

        def l2norm(t):
            return t / jnp.clip(jnp.linalg.norm(t, axis=-1, keepdims=True), 1e-12)

        def rotate_half(x):
            x1, x2 = jnp.split(x, 2, axis=-1)
            return jnp.concatenate([-x2, x1], axis=-1)

        def rotary_xpos(q, k):
            n = q.shape[-2]
            half_idx = jnp.arange(0, DIM_HEAD, 2, dtype=jnp.float32)
            inv_freq = 1.0 / 10000.0 ** (half_idx / DIM_HEAD)
            t = jnp.arange(n, dtype=jnp.float32)
            freqs = t[:, None] * inv_freq[None, :]
            freqs = jnp.concatenate([freqs, freqs], axis=-1)
            base = (half_idx + 0.4 * DIM_HEAD) / (1.4 * DIM_HEAD)
            power = (t - n // 2) / float(WINDOW // 2)
            scale = base[None, :] ** power[:, None]
            scale = jnp.concatenate([scale, scale], axis=-1)
            cos, sin = (jnp.cos(freqs), jnp.sin(freqs))
            q = q * cos * scale + rotate_half(q) * sin * scale
            k = k * cos / scale + rotate_half(k) * sin / scale
            return (q, k)

        def local_attention(q, k, v):
            b, h, n, d = q.shape
            w = n // WINDOW
            bq = q.reshape(b, h, w, WINDOW, d) * QK_SCALE
            bk = k.reshape(b, h, w, WINDOW, d)
            bv = v.reshape(b, h, w, WINDOW, d)

            def look_around(t):
                p = jnp.pad(t, ((0, 0), (0, 0), (1, 0), (0, 0), (0, 0)))
                return jnp.concatenate([p[:, :, :w], p[:, :, 1:]], axis=3)
            bk, bv = (look_around(bk), look_around(bv))
            bt = jnp.arange(n).reshape(w, WINDOW)
            btp = jnp.pad(bt, ((1, 0), (0, 0)), constant_values=-1)
            btk = jnp.concatenate([btp[:w], btp[1:]], axis=1)
            sim = jnp.einsum('bhwid,bhwjd->bhwij', bq, bk)
            i = bt[:, :, None]
            j = btk[:, None, :]
            mask = (i < j) | (i > j + WINDOW) | (j == -1)
            sim = jnp.where(mask, -jnp.finfo(sim.dtype).max, sim)
            attn = jax.nn.softmax(sim, axis=-1)
            out = jnp.einsum('bhwij,bhwjd->bhwid', attn, bv)
            return out.reshape(b, h, n, d)

        def _layer(x, wqkv, qs, ksc, wo, lg, lb, w1, b1, w2, b2):
            b, n, _ = x.shape
            h = shift_token(x)
            qkv = h @ wqkv
            q, k, v = jnp.split(qkv, 3, axis=-1)
            to_heads = lambda t: t.reshape(b, n, HEADS, DIM_HEAD).transpose(0, 2, 1, 3)
            q, k, v = (to_heads(q), to_heads(k), to_heads(v))
            q = l2norm(q) * qs
            k = l2norm(k) * ksc
            q, k = rotary_xpos(q, k)
            o = local_attention(q, k, v)
            o = o.transpose(0, 2, 1, 3).reshape(b, n, INNER)
            x = x + o @ wo
            h = shift_token(x)
            mu = h.mean(-1, keepdims=True)
            var = h.var(-1, keepdims=True)
            h = (h - mu) / jnp.sqrt(var + 1e-05) * lg + lb
            h = h @ w1 + b1
            a, g = jnp.split(h, 2, axis=-1)
            h = a * jax.nn.gelu(g, approximate=False)
            x = x + h @ w2 + b2
            return x
        key = jax.random.key(seed)
        ks = jax.random.split(key, 6)
        return {'x': jax.random.normal(ks[0], (B, N, DIM), jnp.float32), 'wqkv': jax.random.normal(ks[1], (DEPTH, DIM, 3 * INNER), jnp.float32) * 0.02, 'q_scale': jnp.ones((DEPTH, DIM_HEAD), jnp.float32), 'k_scale': jnp.ones((DEPTH, DIM_HEAD), jnp.float32), 'wo': jax.random.normal(ks[2], (DEPTH, INNER, DIM), jnp.float32) * 0.02, 'ln_g': jnp.ones((DEPTH, DIM), jnp.float32), 'ln_b': jnp.zeros((DEPTH, DIM), jnp.float32), 'w1': jax.random.normal(ks[3], (DEPTH, DIM, 2 * HID), jnp.float32) * 0.02, 'b1': jnp.zeros((DEPTH, 2 * HID), jnp.float32), 'w2': jax.random.normal(ks[4], (DEPTH, HID, DIM), jnp.float32) * 0.02, 'b2': jnp.zeros((DEPTH, DIM), jnp.float32)}
    _L0_ffn_in = _L0_ffn_setup()
    _L0_c = _w((lambda *s: np.random.randn(*s).astype(np.float32) * 0.05)(8, 256))
    _L0_wmod = _w((lambda *s: np.random.randn(*s).astype(np.float32) * 0.05)(256, 6 * 256) * 256 ** (-0.5))
    _d = {'L0_attn_x': _L0_attn_in['x'], 'L0_attn_Wq': _L0_attn_in['Wq'], 'L0_attn_bq': _L0_attn_in['bq'], 'L0_attn_Wk': _L0_attn_in['Wk'], 'L0_attn_bk': _L0_attn_in['bk'], 'L0_attn_Wv': _L0_attn_in['Wv'], 'L0_attn_bv': _L0_attn_in['bv'], 'L0_attn_Wp': _L0_attn_in['Wp'], 'L0_attn_bp': _L0_attn_in['bp'], 'L0_ffn_wqkv': _L0_ffn_in['wqkv'], 'L0_ffn_q_scale': _L0_ffn_in['q_scale'], 'L0_ffn_k_scale': _L0_ffn_in['k_scale'], 'L0_ffn_wo': _L0_ffn_in['wo'], 'L0_ffn_ln_g': _L0_ffn_in['ln_g'], 'L0_ffn_ln_b': _L0_ffn_in['ln_b'], 'L0_ffn_w1': _L0_ffn_in['w1'], 'L0_ffn_b1': _L0_ffn_in['b1'], 'L0_ffn_w2': _L0_ffn_in['w2'], 'L0_ffn_b2': _L0_ffn_in['b2'], 'L0_c': _L0_c, 'L0_wmod': _L0_wmod}
    _x0 = _d['L0_attn_x']
    _d['L0_attn_x'] = jax.random.normal(jax.random.fold_in(jax.random.key(seed), 1), (8, 1024, 256), dtype=_x0.dtype)
    del _x0
    return _d

def reference(L0_attn_x, L0_attn_Wq, L0_attn_bq, L0_attn_Wk, L0_attn_bk, L0_attn_Wv, L0_attn_bv, L0_attn_Wp, L0_attn_bp, L0_ffn_wqkv, L0_ffn_q_scale, L0_ffn_k_scale, L0_ffn_wo, L0_ffn_ln_g, L0_ffn_ln_b, L0_ffn_w1, L0_ffn_b1, L0_ffn_w2, L0_ffn_b2, L0_c, L0_wmod):

    def _L0_attn_ref(x, Wq, bq, Wk, bk, Wv, bv, Wp, bp):
        import jax, jax.numpy as jnp
        import numpy as np
        N_HEAD = 16
        W_SCALE = 0.02
        B, T, C = x.shape
        H = N_HEAD
        d = C // H

        def heads(W, b):
            return (jnp.einsum('btc,cd->btd', x, W) + b).reshape(B, T, H, d).transpose(0, 2, 1, 3)
        q = heads(Wq, bq)
        k = heads(Wk, bk)
        v = heads(Wv, bv)
        scale = 1.0 / jnp.sqrt(jnp.asarray(d, x.dtype))
        att = jnp.einsum('bhtd,bhsd->bhts', q, k) * scale
        causal = jnp.tril(jnp.ones((T, T), dtype=bool))
        att = jnp.where(causal[None, None, :, :], att, jnp.asarray(-jnp.inf, att.dtype))
        att = jax.nn.softmax(att, axis=-1)
        y = jnp.einsum('bhts,bhsd->bhtd', att, v)
        y = y.transpose(0, 2, 1, 3).reshape(B, T, C)
        y = jnp.einsum('btc,cd->btd', y, Wp) + bp
        return y

    def _L0_ffn_ref(x, wqkv, q_scale, k_scale, wo, ln_g, ln_b, w1, b1, w2, b2):
        import jax, jax.numpy as jnp
        import numpy as np
        DIM = 256
        DEPTH = 2
        HEADS = 8
        DIM_HEAD = 64
        WINDOW = 128
        INNER = HEADS * DIM_HEAD
        HID = int(DIM * 4 * 2 / 3)
        B, N = (2, 2048)
        QK_SCALE = 8.0

        def shift_token(t):
            t1, t2 = jnp.split(t, 2, axis=-1)
            t2 = jnp.pad(t2, ((0, 0), (1, 0), (0, 0)))[:, :-1]
            return jnp.concatenate([t1, t2], axis=-1)

        def l2norm(t):
            return t / jnp.clip(jnp.linalg.norm(t, axis=-1, keepdims=True), 1e-12)

        def rotate_half(x):
            x1, x2 = jnp.split(x, 2, axis=-1)
            return jnp.concatenate([-x2, x1], axis=-1)

        def rotary_xpos(q, k):
            n = q.shape[-2]
            half_idx = jnp.arange(0, DIM_HEAD, 2, dtype=jnp.float32)
            inv_freq = 1.0 / 10000.0 ** (half_idx / DIM_HEAD)
            t = jnp.arange(n, dtype=jnp.float32)
            freqs = t[:, None] * inv_freq[None, :]
            freqs = jnp.concatenate([freqs, freqs], axis=-1)
            base = (half_idx + 0.4 * DIM_HEAD) / (1.4 * DIM_HEAD)
            power = (t - n // 2) / float(WINDOW // 2)
            scale = base[None, :] ** power[:, None]
            scale = jnp.concatenate([scale, scale], axis=-1)
            cos, sin = (jnp.cos(freqs), jnp.sin(freqs))
            q = q * cos * scale + rotate_half(q) * sin * scale
            k = k * cos / scale + rotate_half(k) * sin / scale
            return (q, k)

        def local_attention(q, k, v):
            b, h, n, d = q.shape
            w = n // WINDOW
            bq = q.reshape(b, h, w, WINDOW, d) * QK_SCALE
            bk = k.reshape(b, h, w, WINDOW, d)
            bv = v.reshape(b, h, w, WINDOW, d)

            def look_around(t):
                p = jnp.pad(t, ((0, 0), (0, 0), (1, 0), (0, 0), (0, 0)))
                return jnp.concatenate([p[:, :, :w], p[:, :, 1:]], axis=3)
            bk, bv = (look_around(bk), look_around(bv))
            bt = jnp.arange(n).reshape(w, WINDOW)
            btp = jnp.pad(bt, ((1, 0), (0, 0)), constant_values=-1)
            btk = jnp.concatenate([btp[:w], btp[1:]], axis=1)
            sim = jnp.einsum('bhwid,bhwjd->bhwij', bq, bk)
            i = bt[:, :, None]
            j = btk[:, None, :]
            mask = (i < j) | (i > j + WINDOW) | (j == -1)
            sim = jnp.where(mask, -jnp.finfo(sim.dtype).max, sim)
            attn = jax.nn.softmax(sim, axis=-1)
            out = jnp.einsum('bhwij,bhwjd->bhwid', attn, bv)
            return out.reshape(b, h, n, d)

        def _layer(x, wqkv, qs, ksc, wo, lg, lb, w1, b1, w2, b2):
            b, n, _ = x.shape
            h = shift_token(x)
            qkv = h @ wqkv
            q, k, v = jnp.split(qkv, 3, axis=-1)
            to_heads = lambda t: t.reshape(b, n, HEADS, DIM_HEAD).transpose(0, 2, 1, 3)
            q, k, v = (to_heads(q), to_heads(k), to_heads(v))
            q = l2norm(q) * qs
            k = l2norm(k) * ksc
            q, k = rotary_xpos(q, k)
            o = local_attention(q, k, v)
            o = o.transpose(0, 2, 1, 3).reshape(b, n, INNER)
            x = x + o @ wo
            h = shift_token(x)
            mu = h.mean(-1, keepdims=True)
            var = h.var(-1, keepdims=True)
            h = (h - mu) / jnp.sqrt(var + 1e-05) * lg + lb
            h = h @ w1 + b1
            a, g = jnp.split(h, 2, axis=-1)
            h = a * jax.nn.gelu(g, approximate=False)
            x = x + h @ w2 + b2
            return x
        for l in range(DEPTH):
            x = _layer(x, wqkv[l], q_scale[l], k_scale[l], wo[l], ln_g[l], ln_b[l], w1[l], b1[l], w2[l], b2[l])
        return x
    x = L0_attn_x
    mod = (_silu(L0_c) @ L0_wmod).reshape(L0_c.shape[0], 6, 1, -1)
    sa, ca, ga, sb, cb, gb = (mod[:, 0], mod[:, 1], mod[:, 2], mod[:, 3], mod[:, 4], mod[:, 5])
    ga = (2 * (ga >= 0) - 1) * jnp.maximum(jnp.abs(ga), 0.25)
    gb = (2 * (gb >= 0) - 1) * jnp.maximum(jnp.abs(gb), 0.25)
    h = _layernorm(x, axis=-1) * (1 + ca) + sa
    x = x + ga * _L0_attn_ref(h, L0_attn_Wq, L0_attn_bq, L0_attn_Wk, L0_attn_bk, L0_attn_Wv, L0_attn_bv, L0_attn_Wp, L0_attn_bp)
    h = _layernorm(x, axis=-1) * (1 + cb) + sb
    x = x + gb * _L0_ffn_ref(h, L0_ffn_wqkv, L0_ffn_q_scale, L0_ffn_k_scale, L0_ffn_wo, L0_ffn_ln_g, L0_ffn_ln_b, L0_ffn_w1, L0_ffn_b1, L0_ffn_w2, L0_ffn_b2)
    return x

_drawn_inputs = setup_inputs


def setup_inputs(seed=0):
    import zlib

    import numpy as np

    out = dict(_drawn_inputs(seed))
    spreads = {'L0_attn_bq': (0.0, 0.8),
     'L0_attn_bk': (0.0, 2.0),
     'L0_attn_bv': (0.0, 0.8),
     'L0_attn_bp': (0.0, 0.317),
     'L0_ffn_q_scale': (1.0, 0.6),
     'L0_ffn_k_scale': (1.0, 0.6),
     'L0_ffn_ln_g': (1.0, 0.6),
     'L0_ffn_ln_b': (0.0, 0.8),
     'L0_ffn_b1': (0.0, 0.8),
     'L0_ffn_b2': (0.0, 0.746)}
    factors = {'L0_attn_Wq': 8.0,
     'L0_attn_Wk': 8.0,
     'L0_attn_Wv': 8.0,
     'L0_attn_Wp': 6.661,
     'L0_ffn_wqkv': 6.849,
     'L0_ffn_wo': 6.74,
     'L0_ffn_w1': 4.769,
     'L0_ffn_w2': 4.75}
    for name, (base, spread) in spreads.items():
        noise = np.random.default_rng([zlib.crc32(name.encode()), seed]).standard_normal(out[name].shape)
        drawn = base * np.exp(spread * noise) if base else spread * noise
        out[name] = jnp.asarray(drawn.astype(out[name].dtype))
    for name, factor in factors.items():
        out[name] = (out[name] * factor).astype(out[name].dtype)
    return out
```

```python
from contextlib import ExitStack

import numpy as np

import concourse.bass as bass
from concourse import mybir

F32 = mybir.dt.float32
F32R = mybir.dt.float32r
BF16 = mybir.dt.bfloat16
ALU = mybir.AluOpType
ACT = mybir.ActivationFunctionType
AX = mybir.AxisListType

P = 128
B, T, C = 8, 1024, 256
TB = T // P
CK = C // P
NMOD = 6
LN_EPS = 1e-5
MASKED = -1e30

H1, D1 = 16, C // 16
G1 = H1 // 4
TERMS_Q = (0, 0, 1, 1, 0, 2)
TERMS_K = (0, 1, 0, 1, 2, 0)
KROWS = len(TERMS_Q) * D1
MROWS = KROWS + 3
VW = 32


def clear(nc, sems):
    with nc.Block() as block:
        @block.gpsimd
        def _(pool):
            for s in sems:
                pool.sem_clear(s)


class Semaphores:

    def __init__(self, nc, ctx):
        self.nc, self.ctx, self.all, self.signals = nc, ctx, [], []

    def enter_context(self, s):
        self.all.append(self.ctx.enter_context(s))
        return self.all[-1]


def prime(nc, signals):
    with nc.Block() as block:
        @block.gpsimd
        def _(pool):
            for s in signals:
                pool.sem_inc(s.sem, 1)


class Signal:

    def __init__(self, sems, nc, name, per, by=1):
        self.sem, self.per, self.by, self.seen = sems.enter_context(nc.semaphore(name)), per, by, 0
        sems.signals.append(self)

    def at(self, i, n):
        return (i * self.per + n) * self.by + 1


class Chain(Signal):

    def start(self, eng, i):
        self.eng, self.i, self.seen = eng, i, 0

    def step(self, ins):
        self.seen += 1
        ins.then_inc(self.sem, 1)
        self.eng.wait_ge(self.sem, self.at(self.i, self.seen))

    def end(self):
        assert self.seen == self.per, (self.seen, self.per)


def newton_rsqrt(eng, chain, y, v, tmp):
    chain.step(eng.tensor_tensor(tmp, y, y, ALU.mult))
    chain.step(eng.scalar_tensor_tensor(out=tmp, in0=tmp, scalar=-0.5, in1=v, op0=ALU.mult, op1=ALU.mult))
    return eng.scalar_tensor_tensor(out=y, in0=tmp, scalar=1.5, in1=y, op0=ALU.add, op1=ALU.mult)


def modulation_stage(nc, sems, c_in, wmod, mod_dram):
    with ExitStack() as ctx:
        sb = lambda name, shape, dt=F32: ctx.enter_context(nc.sbuf_tensor(name, shape, dt))
        ps = lambda name, shape, dt=F32: ctx.enter_context(nc.psum_tensor(name, shape, dt))
        cond = sb("m_cond", [B, C])
        grown = sb("m_grown", [B, C])
        silu = sb("m_silu", [B, C])
        silu_t = sb("m_silu_t", [P, CK, B])
        w = sb("m_w", [P, CK, NMOD * C])
        mod = sb("m_mod", [B, NMOD, C])
        size = sb("m_size", [B, 2, C])
        sign = sb("m_sign", [B, 2, C])
        ident = sb("m_ident", [B, B])
        pt = ps("m_pt", [P, CK, B])
        pm = ps("m_pm", [B, NMOD // 2, 2 * C])
        loaded = sems.enter_context(nc.semaphore("m_loaded"))
        w_loaded = sems.enter_context(nc.semaphore("m_w_loaded"))
        ident_made = sems.enter_context(nc.semaphore("m_ident_made"))
        exp_done = sems.enter_context(nc.semaphore("m_exp_done"))
        turned = sems.enter_context(nc.semaphore("m_turned"))
        silu_done = sems.enter_context(nc.semaphore("m_silu_done"))
        silu_t_done = sems.enter_context(nc.semaphore("m_silu_t_done"))
        product = sems.enter_context(nc.semaphore("m_product"))
        rows_done = sems.enter_context(nc.semaphore("m_rows_done"))
        stored = sems.enter_context(nc.semaphore("m_stored"))
        steps = Chain(sems, nc, "m_steps", 9)
        prime(nc, sems.signals)
        block = ctx.enter_context(nc.Block())

        @block.sync
        def _(sp):
            sp.dma_start(cond[:, :], c_in).then_inc(loaded, 16)
            sp.dma_start(w[:, :, :], wmod.rearrange("(k p) n -> p k n", p=P)).then_inc(w_loaded, 16)
            sp.wait_ge(rows_done, 1)
            sp.dma_start(mod_dram, mod[:, :, :]).then_inc(stored, 16)
            sp.wait_ge(stored, 16)

        @block.gpsimd
        def _(pool):
            pool.memset(ident[:, :], 0.0).then_inc(ident_made, 1)
            pool.wait_ge(ident_made, 1)
            pool.affine_select(out=ident[:, :], in_=ident[:, :], compare_op=ALU.not_equal, fill=1.0,
                               base=0, pattern=[[-1, B]], channel_multiplier=1).then_inc(ident_made, 1)

        @block.scalar
        def _(act):
            act.wait_ge(loaded, 16)
            act.activation(grown[:, :], cond[:, :], ACT.Exp, scale=-1.0).then_inc(exp_done, 1)

        @block.tensor
        def _(pe):
            pe.wait_ge(ident_made, 2)
            pe.wait_ge(silu_done, 1)
            for k in range(CK):
                mm = pe.transpose(pt[:, k, :], silu[:, k * P:(k + 1) * P], ident[:, :])
            mm.then_inc(turned, 1)
            pe.wait_ge(silu_t_done, 1)
            pe.wait_ge(w_loaded, 16)
            for j in range(NMOD // 2):
                for k in range(CK):
                    mm = pe.matmul(pm[:, j, :], silu_t[:, k, :], w[:, k, j * 2 * C:(j + 1) * 2 * C],
                                   start=(k == 0), stop=(k == CK - 1))
            mm.then_inc(product, 1)

        @block.vector
        def _(dve):
            steps.start(dve, 0)
            dve.wait_ge(exp_done, 1)
            steps.step(dve.tensor_scalar(grown[:, :], grown[:, :], 1.0, None, ALU.add))
            steps.step(dve.reciprocal(grown[:, :], grown[:, :]))
            dve.tensor_tensor(silu[:, :], cond[:, :], grown[:, :], ALU.mult).then_inc(silu_done, 1)
            dve.wait_ge(turned, 1)
            dve.tensor_copy(silu_t[:, :, :], pt[:, :, :]).then_inc(silu_t_done, 1)
            dve.wait_ge(product, 1)
            raw = pm[:, :, :].rearrange("b j (r c) -> b (j r) c", r=2)
            steps.step(dve.tensor_copy(mod[:, :, :], raw))
            scales, gates = mod[:, 1:5:3, :], mod[:, 2:6:3, :]
            steps.step(dve.tensor_scalar(scales, scales, 1.0, None, ALU.add))
            steps.step(dve.scalar_tensor_tensor(out=size[:, :, :], in0=gates, scalar=-1.0, in1=gates,
                                                op0=ALU.mult, op1=ALU.max))
            steps.step(dve.tensor_scalar(size[:, :, :], size[:, :, :], 0.25, None, ALU.max))
            steps.step(dve.tensor_scalar(sign[:, :, :], gates, 0.0, 2.0, ALU.is_ge, ALU.mult))
            steps.step(dve.tensor_scalar(sign[:, :, :], sign[:, :, :], 1.0, None, ALU.subtract))
            steps.step(dve.tensor_tensor(gates, size[:, :, :], sign[:, :, :], ALU.mult))
            steps.end()
            dve.tensor_copy(cond[:, 0:1], mod[:, 0, 0:1]).then_inc(rows_done, 1)


def score_steps():
    return [(half, s) for half in range(2) for s in range(4 * half + 4)]


STEPS1 = score_steps()
NSTEP = len(STEPS1)
RING_FILLS = ([("xT", c) for c in range(CK)] + [("qk", m) for m in range(2 * CK)] + [("v", p) for p in range(2)]
              + [("s2", g, n, pair) for g in range(G1) for n in range(NSTEP) for pair in range(2)]
              + [("yT", c) for c in range(CK)] + [("wp", p) for p in range(2)])
RING_AT = {fill: n for n, fill in enumerate(RING_FILLS)}
assert len(RING_FILLS) % 2 == 0

UNITS = [(h, t, piece) for t in range(TB) for h in range(4) for piece in range(t // 4 + 1)]
NUNIT = len(UNITS)
PAIRED = TB // 2
UNIT_COLS = PAIRED + 2 * (TB - PAIRED)
MISC_FILLS = [("mT", 0)]
for _g in range(G1):
    MISC_FILLS += [("oT", _g, 0)] + ([("mT", _g + 1)] if _g + 1 < G1 else []) + [("oT", _g, 1)]
MISC_AT = {fill: n for n, fill in enumerate(MISC_FILLS)}


def unit_col(t, piece):
    return t if t < PAIRED else PAIRED + 2 * (t - PAIRED) + piece


def units_in(n):
    return range(min(NUNIT, 5 * n), min(NUNIT, 5 * (n + 1)))


AT_COPY0, AT_TURN0, AT_COPY1, AT_TURN1, AT_MAX = 4, 6, 0, 1, NSTEP - 1


def attention_stage(nc, sems, x_in, w_in, b_in, mod_dram, x1_dram, f_dram, parts_dram, max_dram, turns):
    with ExitStack() as ctx:
        sb = lambda name, shape, dt=F32: ctx.enter_context(nc.sbuf_tensor(name, shape, dt))
        ps = lambda name, shape, dt=F32: ctx.enter_context(nc.psum_tensor(name, shape, dt))
        sig = lambda name, per, by=1: Signal(sems, nc, name, per, by)
        plain = lambda name: sems.enter_context(nc.semaphore(name))

        NW = 4
        w_hi = sb("a_w_hi", [P, CK, NW, C], F32R)
        w_lo = sb("a_w_lo", [P, CK, NW, C], F32R)
        b_qk = sb("a_b_qk", [P, 2, CK])
        b_v = sb("a_b_v", [P, C])
        b_p = sb("a_b_p", [P, C])
        gate_bp = sb("a_gate_bp", [P, 1, C])
        ident = sb("a_ident", [P, P])
        ident_bf = sb("a_ident_bf", [P, P], BF16)
        mask_ts = sb("a_mask_ts", [P, P], BF16)
        mask_st = sb("a_mask_st", [P, P], BF16)
        modb = sb("a_modb", [P, NMOD - 1, C])
        xl = sb("a_xl", [P, TB, C])
        x1 = sb("a_x1", [P, TB, C])
        stats = sb("a_stats", [P, TB, 6])
        aggr = sb("a_aggr", [P, TB, 2])
        rstd = sb("a_rstd", [P, TB])
        var = sb("a_var", [P, TB])
        var_tmp = sb("a_var_tmp", [P, TB])
        logs = sb("a_logs", [P, TB])
        h_hi = sb("a_h_hi", [P, CK, T], F32R)
        h_lo = sb("a_h_lo", [P, CK, T], F32R)
        qk = sb("a_qk", [P, T])
        qk_part = sb("a_qk_part", [P, 2, 3, T], BF16)
        q_st = sb("a_q_st", [MROWS, H1, T], BF16)
        k_st = sb("a_k_st", [MROWS, H1, T], BF16)
        v_t = sb("a_v_t", [P, TB, H1, VW])
        e_t = sb("a_e_t", [P, 2, 4, 512])
        w_raw = e_t[:, :, :, :].rearrange("p a b (c n) -> p (a b c) n", n=C)[:, 0:CK * NW, :]\
            .rearrange("p (k w) n -> p k w n", k=CK)
        mx = sb("a_mx", [P, 4, UNIT_COLS])
        mx_neg = sb("a_mx_neg", [P, 4, UNIT_COLS])
        nm = sb("a_nm", [P, 4, TB])
        m_rest = sb("a_m_rest", [4 * TB, P])
        m_part = sb("a_m_part", [4 * TB, 3, P], BF16)
        o_un = sb("a_o_un", [P, 512])
        o_rec = sb("a_o_rec", [P, 4, 4])
        y = sb("a_y", [P, TB, C])

        ring = [ps(f"a_ring{n}", [P, 1024]) for n in range(2)]
        unit = [ps(f"a_unit{n}", [P, 512]) for n in range(2)]
        outp = ps("a_outp", [P, 512])
        misc = ps("a_misc", [P, 512])

        NR, NU, NM = len(RING_FILLS), G1 * NUNIT, len(MISC_FILLS)
        NT = len(TERMS_Q)
        w_loaded = plain("a_w_loaded")
        const_made = plain("a_const_made")
        hi_split = plain("a_w_hi_split")
        lo_split = plain("a_w_lo_split")
        x_loaded = sig("a_x_loaded", 1, 16)
        mod_loaded = sig("a_mod_loaded", 1, 16)
        xr_loaded = sig("a_xr_loaded", 1, 16)
        moments = sig("a_moments", 2)
        log_done = sig("a_log_done", 2)
        rstd_near = sig("a_rstd_near", 2)
        normed = sig("a_normed", 2)
        h_ready = sig("a_h_ready", 1)
        ring_full = [sig(f"a_ring_full{n}", NR // 2) for n in range(2)]
        ring_read = [sig(f"a_ring_read{n}", NR // 2) for n in range(2)]
        unit_full = [sig(f"a_unit_full{n}", NU // 2) for n in range(2)]
        unit_read = [sig(f"a_unit_read{n}", NU // 2) for n in range(2)]
        misc_full = sig("a_misc_full", NM)
        misc_read = sig("a_misc_read", NM)
        out_read = sig("a_out_read", 2 * G1)
        hi_done = sig("a_hi_done", 2 * CK)
        qk_split = sig("a_qk_split", 2 * CK)
        parts_stored = [sig(f"a_parts_stored{n}", CK, 16) for n in range(2)]
        stacks_loaded = [sig(f"a_stacks_loaded{g}", 2 * NT, 16) for g in range(G1)]
        nm_done = sig("a_nm_done", G1)
        max_split = sig("a_max_split", G1)
        max_stored = sig("a_max_stored", G1, 16)
        max_loaded = sig("a_max_loaded", G1, 16)
        values_met = sig("a_values_met", G1 * NSTEP)
        biased = sig("a_biased", 1)
        x1_done = sig("a_x1_done", 2)
        f_done = sig("a_f_done", 1)
        x1_stored = sig("a_x1_stored", 1, 16)
        f_stored = sig("a_f_stored", 1, 16)
        dve_steps = Chain(sems, nc, "a_dve_steps", 2 * 5 + 2 * CK * 4 + G1 * 2 + G1 * 3 + 2 * G1)
        pool_steps = Chain(sems, nc, "a_pool_steps", 3)
        prime(nc, sems.signals)
        block = ctx.enter_context(nc.Block())

        def ring_slot(fill):
            n = RING_AT[fill]
            return ring[n % 2], ring_full[n % 2], ring_read[n % 2], n // 2

        def unit_slot(g, u):
            n = g * NUNIT + u
            return unit[n % 2], unit_full[n % 2], unit_read[n % 2], n // 2

        def loop(eng, body):
            if turns == 1:
                body(0)
            else:
                with eng.Fori(0, turns) as i:
                    body(i)

        rows_of = lambda dram, i: dram[i].rearrange("(t p) c -> p t c", p=P)

        @block.sync
        def _(sp):
            sp.dma_start(xl[:, :, :], rows_of(x_in, 0)).then_inc(x_loaded.sem, 16)
            for n in range(NW):
                sp.dma_start(w_raw[:, :, n, :], w_in[n].rearrange("(k p) n -> p k n", p=P)).then_inc(w_loaded, 16)
            with nc.allow_non_contiguous_dma(reason="the biases of q and k go one to a partition"):
                for n in range(2):
                    sp.dma_start(b_qk[:, n, :], b_in[n].rearrange("(m p) -> p m", p=P)).then_inc(w_loaded, 16)
            sp.dma_start(b_v[:, :], b_in[2].partition_broadcast(P)).then_inc(w_loaded, 16)
            sp.dma_start(b_p[:, :], b_in[3].partition_broadcast(P)).then_inc(w_loaded, 16)

            def body(i):
                sp.wait_ge(f_done.sem, f_done.at(i, 0))
                sp.dma_start(modb[:, :, :].rearrange("p r c -> p (r c)"),
                             mod_dram[i, 0:NMOD - 1, :].rearrange("r c -> (r c)").partition_broadcast(P))\
                  .then_inc(mod_loaded.sem, 16)
                for m in range(2 * CK):
                    sp.wait_ge(qk_split.sem, qk_split.at(i, m + 1))
                    sp.dma_start(parts_dram[m // CK][:, (m % CK) * P:(m % CK + 1) * P, :].rearrange("j p t -> p j t"),
                                 qk_part[:, m % 2, :, :]).then_inc(parts_stored[m % 2].sem, 16)
                for n in range(2):
                    sp.wait_ge(parts_stored[n].sem, parts_stored[n].at(i, CK))
                for g in range(G1):
                    for st, terms, w in ((q_st, TERMS_Q, 0), (k_st, TERMS_K, 1)):
                        for j, part in enumerate(terms):
                            sp.dma_start(st[j * D1:(j + 1) * D1, 4 * g:4 * g + 4, :],
                                         parts_dram[w][part, 4 * g * D1:(4 * g + 4) * D1, :]
                                         .rearrange("(h d) t -> d h t", d=D1)).then_inc(stacks_loaded[g].sem, 16)
                sp.wait_ge(x1_stored.sem, x1_stored.at(i, 0))
                sp.dma_start(x1[:, :, :], rows_of(x_in, i)).then_inc(xr_loaded.sem, 16)
                for g in range(G1):
                    sp.wait_ge(max_split.sem, max_split.at(i, g + 1))
                    sp.dma_start(max_dram[g].rearrange("j (r t) -> r j t", t=P), m_part[:, :, :])\
                      .then_inc(max_stored.sem, 16)
                    sp.wait_ge(max_stored.sem, max_stored.at(i, g + 1))
                    sp.dma_start(q_st[KROWS:MROWS, 4 * g:4 * g + 4, :],
                                 max_dram[g].rearrange("j (h t) -> j h t", t=T)).then_inc(max_loaded.sem, 16)
                sp.wait_ge(x1_done.sem, x1_done.at(i, 2))
                sp.dma_start(rows_of(x1_dram, i), x1[:, :, :]).then_inc(x1_stored.sem, 16)
                nxt = 0 if turns == 1 else (i + 1) % turns
                sp.dma_start(xl[:, :, :], rows_of(x_in, nxt)).then_inc(x_loaded.sem, 16)
                sp.wait_ge(f_done.sem, f_done.at(i, 1))
                sp.dma_start(rows_of(f_dram, i), y[:, :, :]).then_inc(f_stored.sem, 16)

            loop(sp, body)
            sp.wait_ge(f_stored.sem, f_stored.at(turns, 0))
            sp.wait_ge(x1_stored.sem, x1_stored.at(turns, 0))
            sp.wait_ge(x_loaded.sem, x_loaded.at(turns, 1))

        @block.gpsimd
        def _(pool):
            pool.memset(ident[:, :], 0.0).then_inc(const_made, 1)
            pool.memset(ident_bf[:, :], 0.0).then_inc(const_made, 1)
            pool.memset(mask_ts[:, :], 0.0).then_inc(const_made, 1)
            pool.memset(mask_st[:, :], 0.0).then_inc(const_made, 1)
            pool.memset(v_t[:, :, :, D1:VW], 0.0).then_inc(const_made, 1)
            pool.wait_ge(const_made, 5)
            pool.memset(v_t[:, :, :, D1:D1 + 1], 1.0).then_inc(const_made, 1)
            pool.wait_ge(const_made, 6)
            pool.memset(k_st[KROWS:MROWS, :, :], 1.0).then_inc(const_made, 1)
            pool.wait_ge(const_made, 7)
            for m in (ident, ident_bf):
                pool.affine_select(out=m[:, :], in_=m[:, :], compare_op=ALU.not_equal, fill=1.0, base=0,
                                   pattern=[[-1, P]], channel_multiplier=1).then_inc(const_made, 1)
            pool.affine_select(out=mask_ts[:, :], in_=mask_ts[:, :], compare_op=ALU.is_ge, fill=MASKED, base=0,
                               pattern=[[-1, P]], channel_multiplier=1).then_inc(const_made, 1)
            pool.affine_select(out=mask_st[:, :], in_=mask_st[:, :], compare_op=ALU.is_ge, fill=MASKED, base=0,
                               pattern=[[1, P]], channel_multiplier=-1).then_inc(const_made, 1)
            pool.wait_ge(w_loaded, 16 * (NW + 4))

            def body(i):
                pool_steps.start(pool, i)
                row = lambda r: modb[:, r:r + 1, :].broadcast_to([P, TB, C])

                pool.wait_ge(mod_loaded.sem, mod_loaded.at(i, 1))
                pool.wait_ge(normed.sem, normed.at(i, 1))
                pool_steps.step(pool.tensor_tensor(xl[:, :, :], xl[:, :, :], row(1), ALU.mult))
                pool.tensor_tensor(xl[:, :, :], xl[:, :, :], row(0), ALU.add).then_inc(h_ready.sem, 1)
                pool.wait_ge(xr_loaded.sem, xr_loaded.at(i, 1))
                pool_steps.step(pool.tensor_tensor(gate_bp[:, 0, :], modb[:, 2, :], b_p[:, :], ALU.mult))
                pool.tensor_tensor(x1[:, :, :], x1[:, :, :], gate_bp[:, :, :].broadcast_to([P, TB, C]),
                                   ALU.add).then_inc(biased.sem, 1)
                pool.wait_ge(biased.sem, biased.at(i, 1))
                for p in range(2):
                    _, _, read, k = ring_slot(("wp", p))
                    pool.wait_ge(read.sem, read.at(i, k + 1))
                    half = slice(4 * p, 4 * p + 4)
                    pool.tensor_tensor(x1[:, half, :], x1[:, half, :], xl[:, half, :], ALU.add)\
                        .then_inc(x1_done.sem, 1)
                pool.wait_ge(normed.sem, normed.at(i, 2))
                pool_steps.step(pool.tensor_tensor(y[:, :, :], y[:, :, :], row(4), ALU.mult))
                pool.tensor_tensor(y[:, :, :], y[:, :, :], row(3), ALU.add).then_inc(f_done.sem, 1)
                pool_steps.end()

            loop(pool, body)

        @block.scalar
        def _(act):
            act.wait_ge(w_loaded, 16 * (NW + 4))
            act.activation(w_hi[:, :, :, :], w_raw, ACT.Copy).then_inc(hi_split, 1)
            act.mul(b_qk[:, 0, :], b_qk[:, 0, :], D1 ** -0.5).then_inc(hi_split, 1)
            act.wait_ge(hi_split, 2)
            act.wait_ge(lo_split, 1)

            def body(i):
                def high(what, before):
                    for c in range(CK):
                        slot, full, _, k = ring_slot((what, c))
                        act.wait_ge(full.sem, full.at(i, k + 1))
                        act.activation(h_hi[:, c, :], slot[:, :], ACT.Copy).then_inc(hi_done.sem, 1)

                def inverse_deviations(which):
                    act.wait_ge(moments.sem, moments.at(i, which + 1))
                    act.activation(logs[:, :], var[:, :], ACT.Ln).then_inc(log_done.sem, 1)
                    act.wait_ge(log_done.sem, log_done.at(i, which + 1))
                    act.activation(rstd[:, :], logs[:, :], ACT.Exp, scale=-0.5).then_inc(rstd_near.sem, 1)

                inverse_deviations(0)
                high("xT", None)
                for m in range(2 * CK):
                    slot, full, read, k = ring_slot(("qk", m))
                    act.wait_ge(full.sem, full.at(i, k + 1))
                    act.wait_ge(qk_split.sem, qk_split.at(i, m))
                    act.activation(qk[:, :], slot[:, :], ACT.Identity, bias=b_qk[:, m // CK, m % CK:m % CK + 1],
                                   scale=D1 ** -0.5 if m < CK else 1.0).then_inc(read.sem, 1)
                for g in range(G1):
                    for n, (half, s) in enumerate(STEPS1):
                        step = g * NSTEP + n
                        for pair in range(2):
                            slot, full, read, k = ring_slot(("s2", g, n, pair))
                            act.wait_ge(full.sem, full.at(i, k + 1))
                            if pair == 0:
                                act.wait_ge(values_met.sem, values_met.at(i, max(step - 1, 0)))
                            cols = 512 * (half + 1) - max(512 * half, P * s)
                            act.activation(e_t[:, step % 2, 2 * pair:2 * pair + 2, 0:cols],
                                           slot[:, :].rearrange("p (h t) -> p h t", h=2)[:, :, 0:cols],
                                           ACT.Exp).then_inc(read.sem, 1)
                high("yT", None)
                inverse_deviations(1)

            loop(act, body)

        @block.tensor
        def _(pe):
            pe.wait_ge(const_made, 11)
            pe.wait_ge(lo_split, 1)

            def body(i):
                def fill(what):
                    slot, full, read, k = ring_slot(what)
                    pe.wait_ge(read.sem, read.at(i, k))
                    return slot, full

                def read_of(what):
                    _, _, read, k = ring_slot(what)
                    pe.wait_ge(read.sem, read.at(i, k + 1))

                def turn_chunks(what, src):
                    for c in range(CK):
                        slot, full = fill((what, c))
                        for t in range(TB):
                            mm = pe.transpose(slot[:, t * P:(t + 1) * P], src[:, t, c * P:(c + 1) * P], ident[:, :])
                        mm.then_inc(full.sem, 1)

                def three(out, lhs, rhs, first, last):
                    for j, (a, b) in enumerate(((0, 0), (0, 1), (1, 0))):
                        mm = pe.matmul(out, lhs[a], rhs[b], start=(first and j == 0), stop=(last and j == 2))
                    return mm

                def project_tokens(what, w):
                    for p in range(2):
                        slot, full = fill((what, p))
                        for t in range(4):
                            tok = slice((4 * p + t) * P, (4 * p + t + 1) * P)
                            for c in range(CK):
                                mm = three(slot[:, t * C:(t + 1) * C], (h_hi[:, c, tok], h_lo[:, c, tok]),
                                           (w_hi[:, c, w, :], w_lo[:, c, w, :]), c == 0, c == CK - 1)
                        mm.then_inc(full.sem, 1)

                def first_pass(g, units):
                    for u in units:
                        h, t, piece = UNITS[u]
                        slot, full, read, k = unit_slot(g, u)
                        pe.wait_ge(read.sem, read.at(i, k))
                        head = 4 * g + h
                        cols = min(512, (t + 1) * P - 512 * piece)
                        diagonal = piece == t // 4
                        mm = pe.matmul(slot[:, 0:cols], q_st[0:KROWS, head, t * P:(t + 1) * P],
                                       k_st[0:KROWS, head, 512 * piece:512 * piece + cols],
                                       start=True, stop=not diagonal)
                        if diagonal:
                            mm = pe.matmul(slot[:, cols - P:cols], ident_bf[:, :], mask_ts[:, :],
                                           start=False, stop=True)
                        mm.then_inc(full.sem, 1)

                def turn_maxima(g):
                    n = MISC_AT[("mT", g)]
                    pe.wait_ge(nm_done.sem, nm_done.at(i, g + 1))
                    pe.wait_ge(misc_read.sem, misc_read.at(i, n))
                    pe.transpose(misc[0:4 * TB, 0:P], nm[:, :, :].rearrange("p h t -> p (h t)"), ident[:, :])\
                      .then_inc(misc_full.sem, 1)

                def scores(g, n, pair):
                    half, s = STEPS1[n]
                    lo = max(512 * half, P * s)
                    cols = 512 * (half + 1) - lo
                    diagonal = P * s >= 512 * half
                    slot, full = fill(("s2", g, n, pair))
                    for hh in range(2):
                        head = 4 * g + 2 * pair + hh
                        mm = pe.matmul(slot[:, 512 * hh:512 * hh + cols], k_st[:, head, s * P:(s + 1) * P],
                                       q_st[:, head, lo:lo + cols], start=True, stop=not diagonal)
                        if diagonal:
                            mm = pe.matmul(slot[:, 512 * hh:512 * hh + P], ident_bf[:, :], mask_st[:, :],
                                           start=False, stop=True)
                    mm.then_inc(full.sem, 1)

                def meet_values(g, n):
                    half, s = STEPS1[n]
                    lo = max(512 * half, P * s) - 512 * half
                    for pair in range(2):
                        read_of(("s2", g, n, pair))
                    if s == 0:
                        pe.wait_ge(out_read.sem, out_read.at(i, 2 * g + half))
                    for h in range(4):
                        mm = pe.matmul(outp[32 * h:32 * h + VW, lo:512], v_t[:, s, 4 * g + h, :],
                                       e_t[:, (g * NSTEP + n) % 2, h, 0:512 - lo],
                                       start=(s == 0), stop=(s == 4 * half + 3))
                    mm.then_inc(values_met.sem, 1)

                def turn_output(g, half):
                    n = MISC_AT[("oT", g, half)]
                    pe.wait_ge(out_read.sem, out_read.at(i, 2 * g + half + 1))
                    pe.wait_ge(misc_read.sem, misc_read.at(i, n))
                    for t in range(4):
                        mm = pe.transpose(misc[:, t * P:(t + 1) * P], o_un[:, t * P:(t + 1) * P], ident[:, :])
                    mm.then_inc(misc_full.sem, 1)

                pe.wait_ge(h_ready.sem, h_ready.at(i, 1))
                turn_chunks("xT", xl)
                for c in range(CK):
                    read_of(("xT", c))
                for m in range(2 * CK):
                    slot, full = fill(("qk", m))
                    w, col = m // CK, slice((m % CK) * P, (m % CK + 1) * P)
                    for half in range(2):
                        tok = slice(512 * half, 512 * half + 512)
                        for c in range(CK):
                            mm = three(slot[:, tok], (w_hi[:, c, w, col], w_lo[:, c, w, col]),
                                       (h_hi[:, c, tok], h_lo[:, c, tok]), c == 0, c == CK - 1)
                    mm.then_inc(full.sem, 1)
                project_tokens("v", 2)
                for g in range(-1, G1):
                    nxt = g + 1
                    if nxt < G1:
                        pe.wait_ge(stacks_loaded[nxt].sem, stacks_loaded[nxt].at(i, 2 * NT))
                    if g < 0:
                        first_pass(0, range(NUNIT))
                        turn_maxima(0)
                        for p in range(2):
                            read_of(("v", p))
                        continue
                    pe.wait_ge(max_loaded.sem, max_loaded.at(i, g + 1))
                    for n in range(NSTEP):
                        units = units_in(n) if nxt < G1 else ()
                        scores(g, n, 0)
                        first_pass(nxt, units[:3])
                        scores(g, n, 1)
                        first_pass(nxt, units[3:])
                        if n > 0:
                            meet_values(g, n - 1)
                        elif g > 0:
                            meet_values(g - 1, NSTEP - 1)
                        if n == AT_TURN0:
                            turn_output(g, 0)
                        if n == AT_TURN1 and g > 0:
                            turn_output(g - 1, 1)
                        if n == AT_MAX and nxt < G1:
                            turn_maxima(nxt)
                meet_values(G1 - 1, NSTEP - 1)
                turn_output(G1 - 1, 1)
                pe.wait_ge(misc_read.sem, misc_read.at(i, NM))
                turn_chunks("yT", y)
                for c in range(CK):
                    read_of(("yT", c))
                project_tokens("wp", 3)

            loop(pe, body)

        @block.vector
        def _(dve):
            dve.wait_ge(hi_split, 1)
            dve.tensor_tensor(w_lo[:, :, :, :], w_raw, w_hi[:, :, :, :].bitcast(F32), ALU.subtract)\
                .then_inc(lo_split, 1)

            def body(i):
                dve_steps.start(dve, i)
                step = dve_steps.step

                def norm(dst, src, which):
                    for t in range(TB):
                        ins = dve.bn_stats(stats[:, t, :], src[:, t, :])
                    step(ins)
                    dve.memset(var_tmp[:, 0:1], 0.0)
                    for t in range(TB):
                        ins = dve.bn_aggr(aggr[:, t, :], stats[:, t, :])
                    step(ins)
                    dve.tensor_scalar(var[:, :], aggr[:, :, 1], LN_EPS, None, ALU.add).then_inc(moments.sem, 1)
                    dve.wait_ge(rstd_near.sem, rstd_near.at(i, which + 1))
                    step(newton_rsqrt(dve, dve_steps, rstd[:, :], var[:, :], var_tmp[:, :]))
                    for t in range(TB):
                        ins = dve.tensor_scalar(dst[:, t, :], src[:, t, :], aggr[:, t, 0:1], rstd[:, t:t + 1],
                                                ALU.subtract, ALU.mult)
                    ins.then_inc(normed.sem, 1)

                def low(what, first):
                    for c in range(CK):
                        slot, _, read, k = ring_slot((what, c))
                        dve.wait_ge(hi_done.sem, hi_done.at(i, first + c + 1))
                        dve.tensor_tensor(h_lo[:, c, :], slot[:, :], h_hi[:, c, :].bitcast(F32), ALU.subtract)\
                           .then_inc(read.sem, 1)

                def reduce_units(g, units):
                    for u in units:
                        h, t, piece = UNITS[u]
                        slot, full, read, k = unit_slot(g, u)
                        cols = min(512, (t + 1) * P - 512 * piece)
                        col = unit_col(t, piece)
                        dve.wait_ge(full.sem, full.at(i, k + 1))
                        dve.reduce_max(mx[:, h, col:col + 1], slot[:, 0:cols], AX.X).then_inc(read.sem, 1)

                def maxima(g):
                    for n in range(2):
                        dve.wait_ge(unit_read[n].sem, unit_read[n].at(i, (g + 1) * NUNIT // 2))
                    step(dve.tensor_scalar(mx_neg[:, :, :], mx[:, :, :], -1.0, None, ALU.mult))
                    step(dve.tensor_copy(nm[:, :, 0:PAIRED], mx_neg[:, :, 0:PAIRED]))
                    dve.tensor_tensor(nm[:, :, PAIRED:TB], mx_neg[:, :, PAIRED:UNIT_COLS:2],
                                      mx_neg[:, :, PAIRED + 1:UNIT_COLS:2], ALU.min).then_inc(nm_done.sem, 1)
                    n = MISC_AT[("mT", g)]
                    dve.wait_ge(misc_full.sem, misc_full.at(i, n + 1))
                    dve.wait_ge(max_stored.sem, max_stored.at(i, g))
                    turned = misc[0:4 * TB, 0:P]
                    step(dve.tensor_copy(m_part[:, 0, :], turned))
                    dve.tensor_tensor(m_rest[:, :], turned, m_part[:, 0, :], ALU.subtract).then_inc(misc_read.sem, 1)
                    dve.wait_ge(misc_read.sem, misc_read.at(i, n + 1))
                    step(dve.tensor_copy(m_part[:, 1, :], m_rest[:, :]))
                    step(dve.tensor_tensor(m_rest[:, :], m_rest[:, :], m_part[:, 1, :], ALU.subtract))
                    dve.tensor_copy(m_part[:, 2, :], m_rest[:, :]).then_inc(max_split.sem, 1)

                def copy_output(g, half):
                    dve.wait_ge(values_met.sem, values_met.at(i, g * NSTEP + (NSTEP if half else 4)))
                    if g or half:
                        dve.wait_ge(misc_full.sem, misc_full.at(i, MISC_AT[("oT", g if half else g - 1, 1 - half)] + 1))
                    dve.tensor_copy(o_un[:, :], outp[:, :]).then_inc(out_read.sem, 1)

                def divide_output(g, half):
                    n = MISC_AT[("oT", g, half)]
                    dve.wait_ge(misc_full.sem, misc_full.at(i, n + 1))
                    o = misc[:, :].rearrange("p (t h d) -> p t h d", t=4, h=4)
                    step(dve.reciprocal(o_rec[:, :, :], o[:, :, :, D1]))
                    dst = y[:, 4 * half:4 * half + 4, 4 * g * D1:(4 * g + 4) * D1]\
                        .rearrange("p t (h d) -> p t h d", h=4)
                    dve.tensor_tensor(dst, o[:, :, :, 0:D1], o_rec[:, :, :].unsqueeze(3).broadcast_to([P, 4, 4, D1]),
                                      ALU.mult).then_inc(misc_read.sem, 1)

                dve.wait_ge(x_loaded.sem, x_loaded.at(i, 1))
                norm(xl, xl, 0)
                low("xT", 0)
                for m in range(2 * CK):
                    _, _, read, k = ring_slot(("qk", m))
                    dve.wait_ge(read.sem, read.at(i, k + 1))
                    stored = parts_stored[m % 2]
                    dve.wait_ge(stored.sem, stored.at(i, m // 2))
                    part = qk_part[:, m % 2, :, :]
                    step(dve.tensor_copy(part[:, 0, :], qk[:, :]))
                    step(dve.tensor_tensor(qk[:, :], qk[:, :], part[:, 0, :], ALU.subtract))
                    step(dve.tensor_copy(part[:, 1, :], qk[:, :]))
                    step(dve.tensor_tensor(qk[:, :], qk[:, :], part[:, 1, :], ALU.subtract))
                    dve.tensor_copy(part[:, 2, :], qk[:, :]).then_inc(qk_split.sem, 1)
                for p in range(2):
                    slot, full, read, k = ring_slot(("v", p))
                    dve.wait_ge(full.sem, full.at(i, k + 1))
                    for t in range(4):
                        ins = dve.tensor_tensor(v_t[:, 4 * p + t, :, 0:D1],
                                                slot[:, t * C:(t + 1) * C].rearrange("p (h d) -> p h d", d=D1),
                                                b_v[:, :].rearrange("p (h d) -> p h d", d=D1), ALU.add)
                    ins.then_inc(read.sem, 1)
                reduce_units(0, range(NUNIT))
                maxima(0)
                dve.wait_ge(f_stored.sem, f_stored.at(i, 0))
                for g in range(G1):
                    nxt = g + 1
                    for n in range(NSTEP):
                        if nxt < G1:
                            reduce_units(nxt, units_in(n))
                        if n == AT_COPY1 and g > 0:
                            copy_output(g - 1, 1)
                        if n == AT_TURN1 and g > 0:
                            divide_output(g - 1, 1)
                        if n == AT_COPY0:
                            copy_output(g, 0)
                        if n == AT_TURN0:
                            divide_output(g, 0)
                        if n == AT_MAX and nxt < G1:
                            maxima(nxt)
                copy_output(G1 - 1, 1)
                divide_output(G1 - 1, 1)
                low("yT", CK)
                for p in range(2):
                    slot, full, read, k = ring_slot(("wp", p))
                    dve.wait_ge(full.sem, full.at(i, k + 1))
                    dve.tensor_tensor(xl[:, 4 * p:4 * p + 4, :], slot[:, :].rearrange("p (t c) -> p t c", c=C),
                                      modb[:, 2:3, :].broadcast_to([P, 4, C]), ALU.mult).then_inc(read.sem, 1)
                dve.wait_ge(x1_done.sem, x1_done.at(i, 2))
                norm(y, x1, 1)
                dve_steps.end()

            loop(dve, body)


H2, D2, WIN = 8, 64, 128
NWIN = T // WIN
PAIRS = H2 // 2
NPP = NWIN * PAIRS
INNER = H2 * D2
HID = C * 4 * 2 // 3
HK = -(-HID // P)
HPAD = HK * P
HLAST = HID - (HK - 1) * P
QK_SCALE = 8.0
NORM_MIN = 1e-12
DRAIN = 6


def rotary_tables():
    f = np.float32
    half = np.arange(0, D2, 2, dtype=f)
    freqs = np.arange(T, dtype=f)[:, None] * (f(1.0) / f(10000.0) ** (half / f(D2)))[None, :]
    base = (half + f(0.4 * D2)) / f(1.4 * D2)
    scale = base[None, :] ** ((np.arange(T, dtype=f) - f(T // 2)) / f(WIN // 2))[:, None]
    two = lambda a, b: np.concatenate([a, b], axis=1).astype(f)
    cos, sin, scale = two(np.cos(freqs), np.cos(freqs)), two(-np.sin(freqs), np.sin(freqs)), two(scale, scale)
    return np.stack([cos * scale, sin * scale, cos / scale, sin / scale]).astype(f)


def plan_fills():
    slots = {name: [] for name in ("qk", "v", "t", "s0", "s1", "et", "ot")}
    for half in range(2):
        slots["et"].append(("fT", half, 0))
        slots["ot"].append(("fT", half, 1))
    slots["qk"].append(("qk", 0))
    slots["v"].append(("v", 0))
    for pp in range(NPP + DRAIN):
        w = pp // PAIRS
        if pp % PAIRS == 0 and pp < NPP:
            if w + 1 < NWIN:
                slots["qk"].append(("qk", w + 1))
                slots["v"].append(("v", w + 1))
            slots["t"] += [("qT", w), ("kT", w)]
        if pp < NPP:
            slots[f"s{pp % 2}"].append(("s", pp))
        if 0 <= pp - 2 < NPP:
            slots["et"].append(("et", pp - 2))
        if 0 <= pp - 3 < NPP and (pp - 3) % PAIRS == 0:
            slots["ot"].append(("oT", (pp - 3) // PAIRS))
        if 0 <= pp - 4 < NPP and (pp - 4) % PAIRS == PAIRS - 1:
            slots["t"].append(("wo", (pp - 4) // PAIRS))
    for half in range(2):
        slots["et"].append(("hT", half, 0))
        slots["ot"].append(("hT", half, 1))
    for half in range(2):
        for m in range(HK):
            if m % 2 == 0:
                slots["qk"].append(("ag", half, m))
            else:
                slots["v"].append(("a", half, m))
                slots["t"].append(("g", half, m))
        for t in range(4):
            slots[f"s{t % 2}"].append(("w2", 4 * half + t))
    return slots


FILLS = plan_fills()
FILL_AT = {f: (name, n, sum(1 for x in fills[:n] if x[0] != "oT"))
           for name, fills in FILLS.items() for n, f in enumerate(fills)}


def layer_stage(nc, sems, pre, f_in, f_out, tables, wqkv, qs, ks, wo, lg, lb, w1, b1, w2, b2, mod_dram, x1_dram, turns,
                final):
    with ExitStack() as ctx:
        sb = lambda name, shape, dt=F32: ctx.enter_context(nc.sbuf_tensor(f"{pre}_{name}", shape, dt))
        ps = lambda name, shape, dt=F32: ctx.enter_context(nc.psum_tensor(f"{pre}_{name}", shape, dt))
        sig = lambda name, per, by=1: Signal(sems, nc, f"{pre}_{name}", per, by)
        plain = lambda name: sems.enter_context(nc.semaphore(f"{pre}_{name}"))

        part = lambda name, shape: [sb(f"{name}_{x}", shape, F32R) for x in ("hi", "lo")]
        wqkv_p = part("wqkv", [P, CK, 3 * INNER])
        wo_p = part("wo", [P, PAIRS, C])
        w1_p = part("w1", [P, CK, 2, HPAD])
        w2_p = part("w2", [P, HK, C])
        tab = sb("tab", [P, 2, 2, NWIN, D2])
        qk_scale = sb("qk_scale", [P, 2, D2])
        ln_g = sb("ln_g", [P, CK])
        ln_b = sb("ln_b", [P, CK])
        b1_c = sb("b1_c", [P, 2, HK])
        b2_r = sb("b2_r", [P, 1, C])
        gate_r = sb("gate_r", [P, 1, C])
        ident = sb("ident", [P, P])
        ident_bf = sb("ident_bf", [P, P], BF16)
        mask = sb("mask", [P, 2, 2 * WIN], BF16)
        half_log = sb("half_log", [P, 1])

        fl = sb("fl", [P, TB, C])
        fr = sb("fr", [P, TB, C])
        hn = sb("hn", [P, TB, C])
        hs = sb("hs", [P, TB, P])
        turned = part("turned", [P, CK, T + 2])
        qk = sb("qk", [P, 2, H2, D2])
        sq = sb("sq", [P, 2 * H2, D2])
        rot = sb("rot", [P, 2, H2, D2])
        qk_rot = sb("qk_rot", [P, 2, H2, D2])
        sums = sb("sums", [P, NWIN, 2 * H2])
        logs = sb("logs", [P, NWIN, 2 * H2])
        inv = sb("inv", [P, NWIN, 2 * H2])
        inv_tmp = sb("inv_tmp", [P, 2 * H2])
        scale_q = sb("scale_q", [P, NWIN, H2])
        v = sb("v", [P, 4, H2, D2])
        q_t = sb("q_t", [P, PAIRS, WIN])
        k_t = sb("k_t", [P, 2, H2, WIN])
        top = sb("top", [P, NPP, 2])
        bias = sb("bias", [P, NPP, 2])
        total = sb("total", [P, NPP, 2])
        share = sb("share", [P, NPP, 2])
        e = sb("e", [P, 3, 2, 2 * WIN])
        e_t = sb("e_t", [P, 2, 4, WIN])
        o_p = part("o", [P, PAIRS, WIN])
        stats = sb("stats", [P, TB, 2, 6])
        aggr = sb("aggr", [P, TB, 2])
        var = sb("var", [P, TB])
        var_tmp = sb("var_tmp", [P, TB])
        var_log = sb("var_log", [P, TB])
        rstd = sb("rstd", [P, TB])
        gelu = sb("gelu", [P, 2, 512])
        wide = sb("wide", [P, 2, 512])
        hid_p = part("hid", [P, HK, 512])
        stage = [fr[:, :, :].rearrange("p t c -> p (t c)"), hn[:, :, :].rearrange("p t c -> p (t c)")]

        bank = {name: ps("bank_" + name, [P, 1024 if name == "qk" else 512]) for name in FILLS}
        full = {n: sig(f"full_{n}", sum(1 for f in fills if f[0] != "oT")) for n, fills in FILLS.items()}
        read = {n: sig(f"read_{n}", len(fills)) for n, fills in FILLS.items()}

        const_made = plain("const_made")
        stage_zero = plain("stage_zero")
        raw_loaded = [plain(f"raw_loaded{n}") for n in range(3)]
        hi_split = plain("hi_split")
        lo_split = plain("lo_split")
        small_loaded = plain("small_loaded")
        tab_made = plain("tab_made")
        f_loaded = sig("f_loaded", 1, 16)
        gate_loaded = sig("gate_loaded", 1, 16)
        x1_loaded = sig("x1_loaded", 1, 16)
        f_hi = sig("f_hi", 4)
        squared = sig("squared", NWIN)
        qk_copied = sig("qk_copied", NWIN)
        summed = sig("summed", NWIN)
        logged = sig("logged", NWIN)
        inv_near = sig("inv_near", NWIN)
        inv_done = sig("inv_done", NWIN)
        turned_parts = sig("turned_parts", NWIN)
        q_rotated = sig("q_rotated", NWIN)
        rotated = sig("rotated", NWIN)
        bias_done = sig("bias_done", NPP)
        exp_done = sig("exp_done", NPP)
        share_done = sig("share_done", NPP)
        e_done = sig("e_done", NPP)
        pairs_met = sig("pairs_met", NPP)
        o_hi = sig("o_hi", NWIN)
        shifted = sig("shifted", 2 * NWIN - 1, 16)
        moments = sig("moments", 1)
        var_logged = sig("var_logged", 1)
        rstd_near = sig("rstd_near", 1)
        normed = sig("normed", 1)
        h_hi = sig("h_hi", 4)
        h_lo = sig("h_lo", 4)
        gelu_done = sig("gelu_done", HK)
        hid_hi = sig("hid_hi", 2 * HK)
        hid_lo = sig("hid_lo", 2 * HK)
        b2_added = sig("b2_added", 1)
        gated = sig("gated", 1)
        finished = sig("finished", 1)
        f_stored = sig("f_stored", 1, 16)
        dve_steps = Chain(sems, nc, f"{pre}_dve_steps", 4 * NWIN + NPP + 5)
        prime(nc, sems.signals)
        block = ctx.enter_context(nc.Block())

        def loop(eng, body):
            if turns == 1:
                body(0)
            else:
                with eng.Fori(0, turns) as i:
                    body(i)

        rows_of = lambda dram, i: dram[i].rearrange("(t p) c -> p t c", p=P)
        w1_view = lambda st: st[:, 0:2 * HPAD].rearrange("p (a n) -> p a n", a=2)
        w2_tail = hs[:, 0:2, :].rearrange("p t c -> p (t c)")
        pieces = [(n, w1_view(stage[n]), w1_p[0][:, n, :, :], w1_p[1][:, n, :, :]) for n in range(CK)]
        pieces += [(2, w2_tail, w2_p[0][:, HK - 1, :], w2_p[1][:, HK - 1, :])]
        pieces += [(n, stage[n][:, 0:3 * INNER], wqkv_p[0][:, n, :], wqkv_p[1][:, n, :]) for n in range(CK)]
        pieces += [(0, stage[0][:, 0:PAIRS * C].rearrange("p (k c) -> p k c", c=C), wo_p[0][:, :, :], wo_p[1][:, :, :]),
                   (1, stage[1][:, 0:(HK - 1) * C].rearrange("p (k c) -> p k c", c=C),
                    w2_p[0][:, 0:HK - 1, :], w2_p[1][:, 0:HK - 1, :])]
        n_loads = {0: 2, 1: 2, 2: 1, 3: 1, 4: 1, 5: 1, 6: 1}
        arrived = []
        for n, piece in enumerate(pieces):
            before = sum(n_loads[k] for k in range(n) if pieces[k][0] == piece[0])
            arrived.append(16 * (before + n_loads[n]))
        NSMALL = 4 + 2 + 2 + 4 + 1

        @block.sync
        def _(sp):
            sp.wait_ge(stage_zero, 4)
            for n in range(CK):
                for a in range(2):
                    sp.dma_start(w1_view(stage[n])[:, a, 0:HID], w1[n * P:(n + 1) * P, a * HID:(a + 1) * HID])\
                      .then_inc(raw_loaded[n], 16)
            sp.dma_start(w2_tail[0:HLAST, :], w2[(HK - 1) * P:HID, :]).then_inc(raw_loaded[2], 16)
            sp.dma_start(fl[:, :, :], rows_of(f_in, 0)).then_inc(f_loaded.sem, 16)
            for n in range(4):
                sp.dma_start(tab[:, n // 2, n % 2, :, :], tables[n].rearrange("(w p) d -> p w d", p=P))\
                  .then_inc(small_loaded, 16)
            sp.dma_start(qk_scale[:, 0, :], qs.partition_broadcast(P)).then_inc(small_loaded, 16)
            sp.dma_start(qk_scale[:, 1, :], ks.partition_broadcast(P)).then_inc(small_loaded, 16)
            with nc.allow_non_contiguous_dma(reason="vectors that go one value to a partition"):
                sp.dma_start(ln_g[:, :], lg.rearrange("(k p) -> p k", p=P)).then_inc(small_loaded, 16)
                sp.dma_start(ln_b[:, :], lb.rearrange("(k p) -> p k", p=P)).then_inc(small_loaded, 16)
                for a in range(2):
                    sp.dma_start(b1_c[:, a, 0:HK - 1], b1[a * HID:a * HID + (HK - 1) * P]
                                 .rearrange("(m p) -> p m", p=P)).then_inc(small_loaded, 16)
                    sp.dma_start(b1_c[0:HLAST, a, HK - 1:HK], b1[a * HID + (HK - 1) * P:(a + 1) * HID]
                                 .rearrange("(p m) -> p m", m=1)).then_inc(small_loaded, 16)
            sp.dma_start(b2_r[:, 0, :], b2.partition_broadcast(P)).then_inc(small_loaded, 16)
            later = {3: wqkv[0:P, :], 4: wqkv[P:C, :], 5: wo.rearrange("(k p) c -> p k c", p=P),
                     6: w2[0:(HK - 1) * P, :].rearrange("(k p) c -> p k c", p=P)}
            for n, src in later.items():
                sp.wait_ge(lo_split, 1 + max(m for m in range(n) if pieces[m][0] == pieces[n][0]))
                sp.dma_start(pieces[n][1], src).then_inc(raw_loaded[pieces[n][0]], 16)

            def body(i):
                for w in range(NWIN):
                    _, n, _ = FILL_AT[("wo", w)]
                    sp.wait_ge(read["t"].sem, read["t"].at(i, n + 1))
                    sp.dma_start(hs[1:P, w, :], fr[0:P - 1, w, P:C]).then_inc(shifted.sem, 16)
                    if w:
                        sp.dma_start(hs[0:1, w, :], fr[P - 1:P, w - 1, P:C]).then_inc(shifted.sem, 16)
                nxt = 0 if turns == 1 else (i + 1) % turns
                sp.dma_start(fl[:, :, :], rows_of(f_in, nxt)).then_inc(f_loaded.sem, 16)
                if final:
                    name, _, k = FILL_AT[("hT", 1, 1)]
                    sp.wait_ge(full[name].sem, full[name].at(i, k + 1))
                    sp.dma_start(hn[:, :, :], rows_of(x1_dram, i)).then_inc(x1_loaded.sem, 16)
                    sp.dma_start(gate_r[:, 0, :], mod_dram[i, NMOD - 1, :].partition_broadcast(P))\
                      .then_inc(gate_loaded.sem, 16)
                    sp.wait_ge(finished.sem, finished.at(i, 1))
                for name in ("s0", "s1"):
                    sp.wait_ge(read[name].sem, read[name].at(i, len(FILLS[name])))
                sp.dma_start(rows_of(f_out, i), fr[:, :, :]).then_inc(f_stored.sem, 16)

            loop(sp, body)
            sp.wait_ge(f_stored.sem, f_stored.at(turns, 0))
            sp.wait_ge(f_loaded.sem, f_loaded.at(turns, 1))

        @block.gpsimd
        def _(pool):
            pool.memset(stage[0], 0.0).then_inc(stage_zero, 1)
            pool.memset(stage[1], 0.0).then_inc(stage_zero, 1)
            pool.memset(hs[:, :, :], 0.0).then_inc(stage_zero, 1)
            pool.memset(b1_c[:, :, :], 0.0).then_inc(stage_zero, 1)
            pool.memset(ident[:, :], 0.0).then_inc(const_made, 1)
            pool.memset(ident_bf[:, :], 0.0).then_inc(const_made, 1)
            pool.memset(mask[:, :, :], 0.0).then_inc(const_made, 1)
            pool.memset(k_t[:, :, :, :], 0.0).then_inc(const_made, 1)
            for t in turned:
                pool.memset(t[:, :, 0:1].bitcast(F32), 0.0).then_inc(const_made, 1)
            pool.memset(half_log[:, :], 8 * float(np.log(2.0))).then_inc(const_made, 1)
            pool.wait_ge(const_made, 7)
            for m in (ident, ident_bf):
                pool.affine_select(out=m[:, :], in_=m[:, :], compare_op=ALU.not_equal, fill=1.0, base=0,
                                   pattern=[[-1, P]], channel_multiplier=1).then_inc(const_made, 1)
            pool.affine_select(out=mask[:, :, 0:WIN], in_=mask[:, :, 0:WIN], compare_op=ALU.is_ge, fill=MASKED,
                               base=0, pattern=[[0, 2], [1, WIN]], channel_multiplier=-1).then_inc(const_made, 1)
            pool.affine_select(out=mask[:, :, WIN:2 * WIN], in_=mask[:, :, WIN:2 * WIN], compare_op=ALU.is_ge,
                               fill=MASKED, base=0, pattern=[[0, 2], [-1, WIN]], channel_multiplier=1)\
                .then_inc(const_made, 1)
            pool.wait_ge(lo_split, 3)
            pool.memset(hs[0:1, 0, :], 0.0).then_inc(const_made, 1)
            pool.wait_ge(small_loaded, 16 * NSMALL)

            def body(i):

                def rotate(w):
                    pool.wait_ge(turned_parts.sem, turned_parts.at(i, w + 1))
                    pool.tensor_tensor(qk_rot[:, :, :, :], qk_rot[:, :, :, :], rot[:, :, :, :], ALU.add)\
                        .then_inc(q_rotated.sem, 1)
                    pool.wait_ge(q_rotated.sem, q_rotated.at(i, w + 1))
                    pool.wait_ge(inv_done.sem, inv_done.at(i, w + 1))
                    pool.tensor_tensor(qk_rot[:, 1, :, :], qk_rot[:, 1, :, :],
                                       inv[:, w, H2:2 * H2].unsqueeze(2).broadcast_to([P, H2, D2]), ALU.mult)\
                        .then_inc(rotated.sem, 1)

                def share_out(pp):
                    lo = WIN if pp < PAIRS else 0
                    pool.wait_ge(share_done.sem, share_done.at(i, pp + 1))
                    weights = e[:, pp % 3, :, lo:]
                    pool.tensor_tensor(weights, weights, share[:, pp, :].unsqueeze(2)
                                       .broadcast_to([P, 2, 2 * WIN - lo]), ALU.mult).then_inc(e_done.sem, 1)

                rotate(0)
                for pp in range(NPP):
                    share_out(pp)
                    if pp % PAIRS == 2 and pp // PAIRS + 1 < NWIN:
                        rotate(pp // PAIRS + 1)
                for n in range(4):
                    half, c = n // 2, n % 2
                    pool.wait_ge(h_hi.sem, h_hi.at(i, n + 1))
                    cols = slice(1 + 512 * half, 513 + 512 * half)
                    pool.tensor_tensor(turned[1][:, c, cols], wide[:, n % 2, :], turned[0][:, c, cols].bitcast(F32),
                                       ALU.subtract).then_inc(h_lo.sem, 1)
                pool.wait_ge(normed.sem, normed.at(i, 1))
                pool.tensor_tensor(fr[:, :, :], fr[:, :, :], b2_r[:, :, :].broadcast_to([P, TB, C]), ALU.add)\
                    .then_inc(b2_added.sem, 1)
                for n in range(2 * HK):
                    m = n % HK
                    pool.wait_ge(hid_hi.sem, hid_hi.at(i, n + 1))
                    pool.tensor_tensor(hid_p[1][:, m, :], wide[:, n % 2, :], hid_p[0][:, m, :].bitcast(F32),
                                       ALU.subtract).then_inc(hid_lo.sem, 1)
                if final:
                    for name in ("s0", "s1"):
                        pool.wait_ge(read[name].sem, read[name].at(i, len(FILLS[name])))
                    pool.wait_ge(gate_loaded.sem, gate_loaded.at(i, 1))
                    pool.wait_ge(x1_loaded.sem, x1_loaded.at(i, 1))
                    pool.tensor_tensor(fr[:, :, :], fr[:, :, :], gate_r[:, :, :].broadcast_to([P, TB, C]), ALU.mult)\
                        .then_inc(gated.sem, 1)
                    pool.wait_ge(gated.sem, gated.at(i, 1))
                    pool.tensor_tensor(fr[:, :, :], fr[:, :, :], hn[:, :, :], ALU.add).then_inc(finished.sem, 1)

            loop(pool, body)

        @block.scalar
        def _(act):
            for n, (buf, raw, hi, lo) in enumerate(pieces):
                act.wait_ge(raw_loaded[buf], arrived[n])
                act.activation(hi, raw, ACT.Copy).then_inc(hi_split, 1)
            act.wait_ge(const_made, 11)
            act.wait_ge(small_loaded, 16 * NSMALL)

            def body(i):
                def wait_full(what):
                    name, n, k = FILL_AT[what]
                    act.wait_ge(full[name].sem, full[name].at(i, k + 1))
                    return bank[name], read[name].sem

                def take_window(w):
                    src, back = wait_full(("qk", w))
                    if w:
                        act.wait_ge(turned_parts.sem, turned_parts.at(i, w))
                    act.activation(qk[:, :, :, :].rearrange("p a h d -> p (a h d)"), src[:, :], ACT.Copy)\
                        .then_inc(back, 1)
                    _, n, _ = FILL_AT[("qk", w)]
                    act.wait_ge(back, read["qk"].at(i, n + 1))
                    if w:
                        act.wait_ge(summed.sem, summed.at(i, w))
                    act.activation(sq[:, :, :].rearrange("p h d -> p (h d)"),
                                   qk[:, :, :, :].rearrange("p a h d -> p (a h d)"), ACT.Square)\
                        .then_inc(squared.sem, 1)
                    src, back = wait_full(("v", w))
                    if w >= 4:
                        act.wait_ge(pairs_met.sem, pairs_met.at(i, PAIRS * (w - 2)))
                    act.activation(v[:, w % 4, :, :].rearrange("p h d -> p (h d)"), src[:, :], ACT.Copy)\
                        .then_inc(back, 1)

                def inverse_norms(w):
                    act.wait_ge(summed.sem, summed.at(i, w + 1))
                    act.activation(logs[:, w, :], sums[:, w, :], ACT.Ln, scale=65536.0).then_inc(logged.sem, 1)
                    act.wait_ge(logged.sem, logged.at(i, w + 1))
                    act.activation(inv[:, w, :], logs[:, w, :], ACT.Exp, scale=-0.5, bias=half_log[:, :])\
                        .then_inc(inv_near.sem, 1)

                for half in range(2):
                    for c in range(CK):
                        src, _ = wait_full(("fT", half, c))
                        act.activation(turned[0][:, c, 1 + 512 * half:513 + 512 * half], src[:, :], ACT.Copy)\
                            .then_inc(f_hi.sem, 1)
                take_window(0)
                inverse_norms(0)
                for pp in range(NPP + DRAIN):
                    w = pp // PAIRS
                    if pp % PAIRS == 0 and w + 1 < NWIN:
                        take_window(w + 1)
                    if pp < NPP:
                        src, back = wait_full(("s", pp))
                        act.wait_ge(bias_done.sem, bias_done.at(i, pp + 1))
                        if pp >= 3:
                            _, _, k = FILL_AT[("et", pp - 3)]
                            act.wait_ge(full["et"].sem, full["et"].at(i, k + 1))
                        lo = WIN if w == 0 else 0
                        for hh in range(2):
                            h = 2 * (pp % PAIRS) + hh
                            ins = act.activation(e[:, pp % 3, hh, lo:], src[:, 2 * WIN * hh + lo:2 * WIN * (hh + 1)],
                                                 ACT.Exp, scale=scale_q[:, w, h:h + 1], bias=bias[:, pp, hh:hh + 1],
                                                 accum_out=total[:, pp, hh:hh + 1])
                        ins.then_inc(back, 1)
                    if pp % PAIRS == 1 and w + 1 < NWIN:
                        inverse_norms(w + 1)
                    if 0 <= pp - 2 < NPP and pp % 2 == 0:
                        take_turned(act, i, pp - 2)
                    if 0 <= pp - 3 < NPP and (pp - 3) % PAIRS == PAIRS - 1:
                        wo_w = (pp - 3) // PAIRS
                        act.wait_ge(pairs_met.sem, pairs_met.at(i, PAIRS * (wo_w + 1)))
                        if wo_w:
                            _, _, k = FILL_AT[("wo", wo_w - 1)]
                            act.wait_ge(full["t"].sem, full["t"].at(i, k + 1))
                        act.activation(o_p[0][:, :, :].rearrange("p a t -> p (a t)"), bank["ot"][:, :], ACT.Copy)\
                            .then_inc(o_hi.sem, 1)
                act.wait_ge(moments.sem, moments.at(i, 1))
                act.activation(var_log[:, :], var[:, :], ACT.Ln).then_inc(var_logged.sem, 1)
                act.wait_ge(var_logged.sem, var_logged.at(i, 1))
                act.activation(rstd[:, :], var_log[:, :], ACT.Exp, scale=-0.5).then_inc(rstd_near.sem, 1)
                for n in range(4):
                    half, c = n // 2, n % 2
                    name, k, _ = FILL_AT[("hT", half, c)]
                    act.wait_ge(read[name].sem, read[name].at(i, k + 1))
                    act.activation(turned[0][:, c, 1 + 512 * half:513 + 512 * half], wide[:, n % 2, :], ACT.Copy)\
                        .then_inc(h_hi.sem, 1)
                for n in range(2 * HK):
                    half, m = n // HK, n % HK
                    src, back = wait_full(("g", half, m) if m % 2 else ("ag", half, m))
                    if n >= 2:
                        name, k, _ = FILL_AT[("a" if m % 2 else "ag", (n - 2) // HK, (n - 2) % HK)]
                        act.wait_ge(read[name].sem, read[name].at(i, k + 1))
                    act.activation(gelu[:, n % 2, :], src[:, 0 if m % 2 else 512:], ACT.Gelu,
                                   bias=b1_c[:, 1, m:m + 1]).then_inc(back if m % 2 else gelu_done.sem, 1)

            def take_turned(eng, i, pp):
                name, n, k = FILL_AT[("et", pp)]
                eng.wait_ge(full[name].sem, full[name].at(i, k + 1))
                if pp >= 2:
                    eng.wait_ge(pairs_met.sem, pairs_met.at(i, pp - 1))
                lo = 1 if pp < PAIRS else 0
                dst = e_t[:, pp % 2, :, :].rearrange("p (h b) t -> p h b t", h=2)[:, :, lo:, :]
                src = bank[name][:, :].rearrange("p (h b t) -> p h b t", h=2, b=2)[:, :, lo:, :]
                eng.activation(dst, src, ACT.Copy).then_inc(read[name].sem, 1)

            loop(act, body)

        @block.tensor
        def _(pe):
            pe.wait_ge(const_made, 11)
            pe.wait_ge(lo_split, len(pieces))

            def body(i):
                def fill(what):
                    name, n, _ = FILL_AT[what]
                    pe.wait_ge(read[name].sem, read[name].at(i, n))
                    return bank[name], full[name].sem

                def read_of(what):
                    name, n, _ = FILL_AT[what]
                    pe.wait_ge(read[name].sem, read[name].at(i, n + 1))

                def three(out, lhs, rhs, first, last):
                    for j, (a, b) in enumerate(((0, 0), (0, 1), (1, 0))):
                        mm = pe.matmul(out, lhs(a), rhs(b), start=(first and j == 0), stop=(last and j == 2))
                    return mm

                def turn_rows(what, src):
                    for half in range(2):
                        for c in range(CK):
                            slot, done = fill((what, half, c))
                            for t in range(4):
                                mm = pe.transpose(slot[:, t * P:(t + 1) * P], src[:, 4 * half + t, c * P:(c + 1) * P],
                                                  ident[:, :])
                            mm.then_inc(done, 1)

                def project(w):
                    for what, cols, n0 in ((("qk", w), 2, 0), (("v", w), 1, 2)):
                        slot, done = fill(what)
                        for j in range(cols):
                            out = slot[:, 512 * j:512 * (j + 1)]
                            for c in range(CK):
                                tok = slice(w * WIN + 1 - c, (w + 1) * WIN + 1 - c)
                                mm = three(out, lambda a: turned[a][:, c, tok],
                                           lambda b: wqkv_p[b][:, c, 512 * (n0 + j):512 * (n0 + j + 1)],
                                           c == 0, c == CK - 1)
                        mm.then_inc(done, 1)

                def turn_qk(w):
                    pe.wait_ge(rotated.sem, rotated.at(i, w + 1))
                    for a, what in enumerate(("qT", "kT")):
                        slot, done = fill((what, w))
                        for p in range(PAIRS):
                            mm = pe.transpose(slot[:, p * P:(p + 1) * P],
                                              qk_rot[:, a, 2 * p:2 * p + 2, :].rearrange("p h d -> p (h d)"),
                                              ident[:, :])
                        mm.then_inc(done, 1)

                def scores(pp):
                    w, p = pp // PAIRS, pp % PAIRS
                    if p == 0:
                        read_of(("kT", w))
                    slot, done = fill(("s", pp))
                    for hh in range(2):
                        for b in range(1 if w == 0 else 0, 2):
                            at = (2 * hh + b) * WIN
                            mm = pe.matmul(slot[:, at:at + WIN], q_t[:, p, :], k_t[:, (w - 1 + b) % 2, 2 * p + hh, :],
                                           start=True, stop=False)
                            mm = pe.matmul(slot[:, at:at + WIN], ident_bf[:, :], mask[:, hh, b * WIN:(b + 1) * WIN],
                                           start=False, stop=True)
                    mm.then_inc(done, 1)

                def turn_weights(pp):
                    pe.wait_ge(e_done.sem, e_done.at(i, pp + 1))
                    slot, done = fill(("et", pp))
                    for hh in range(2):
                        for b in range(1 if pp < PAIRS else 0, 2):
                            at = (2 * hh + b) * WIN
                            mm = pe.transpose(slot[:, at:at + WIN], e[:, pp % 3, hh, b * WIN:(b + 1) * WIN],
                                              ident[:, :])
                    mm.then_inc(done, 1)

                def meet_values(pp):
                    w, p = pp // PAIRS, pp % PAIRS
                    read_of(("et", pp))
                    if p == 0:
                        slot, _ = fill(("oT", w))
                        read_of(("v", w))
                    first = 1 if w == 0 else 0
                    for hh in range(2):
                        for b in range(first, 2):
                            mm = pe.matmul(bank["ot"][D2 * hh:D2 * (hh + 1), p * WIN:(p + 1) * WIN],
                                           v[:, (w - 1 + b) % 4, 2 * p + hh, :], e_t[:, pp % 2, 2 * hh + b, :],
                                           start=(b == first), stop=(b == 1))
                    mm.then_inc(pairs_met.sem, 1)

                def project_out(w):
                    read_of(("oT", w))
                    slot, done = fill(("wo", w))
                    for p in range(PAIRS):
                        mm = three(slot[:, 0:C], lambda a: o_p[a][:, p, :], lambda b: wo_p[b][:, p, :],
                                   p == 0, p == PAIRS - 1)
                    mm.then_inc(done, 1)

                pe.wait_ge(f_loaded.sem, f_loaded.at(i, 1))
                turn_rows("fT", fl)
                read_of(("fT", 1, 0))
                read_of(("fT", 1, 1))
                project(0)
                for pp in range(NPP + DRAIN):
                    if pp % PAIRS == 0 and pp < NPP:
                        w = pp // PAIRS
                        if w + 1 < NWIN:
                            project(w + 1)
                        turn_qk(w)
                    if pp < NPP:
                        scores(pp)
                    if 0 <= pp - 2 < NPP:
                        turn_weights(pp - 2)
                    if 0 <= pp - 3 < NPP:
                        meet_values(pp - 3)
                    if 0 <= pp - 4 < NPP and (pp - 4) % PAIRS == PAIRS - 1:
                        project_out((pp - 4) // PAIRS)
                pe.wait_ge(normed.sem, normed.at(i, 1))
                turn_rows("hT", hn)
                for half in range(2):
                    pe.wait_ge(h_lo.sem, h_lo.at(i, 2 * half + 2))
                    tok = slice(1 + 512 * half, 513 + 512 * half)
                    for m in range(HK):
                        targets = (("a", half, m), ("g", half, m)) if m % 2 else (("ag", half, m),)
                        slots = [fill(x) for x in targets]
                        for a in range(2):
                            out = slots[a][0][:, :] if m % 2 else slots[0][0][:, 512 * a:512 * (a + 1)]
                            for c in range(CK):
                                mm = three(out, lambda b: w1_p[b][:, c, a, m * P:(m + 1) * P],
                                           lambda b: turned[b][:, c, tok], c == 0, c == CK - 1)
                            if m % 2 or a == 1:
                                mm.then_inc(slots[a if m % 2 else 0][1], 1)
                    for t in range(4):
                        slot, done = fill(("w2", 4 * half + t))
                        for m in range(HK):
                            if t == 0:
                                pe.wait_ge(hid_lo.sem, hid_lo.at(i, half * HK + m + 1))
                            mm = three(slot[:, 0:C], lambda a: hid_p[a][:, m, t * P:(t + 1) * P],
                                       lambda b: w2_p[b][:, m, :], m == 0, m == HK - 1)
                        mm.then_inc(done, 1)

            loop(pe, body)

        @block.vector
        def _(dve):
            for n, (buf, raw, hi, lo) in enumerate(pieces):
                dve.wait_ge(hi_split, n + 1)
                dve.tensor_tensor(lo, raw, hi.bitcast(F32), ALU.subtract).then_inc(lo_split, 1)
            dve.wait_ge(small_loaded, 16 * NSMALL)
            for a in range(2):
                s = qk_scale[:, a, :].rearrange("p (r d) -> p r d", r=2)
                for r, view in ((0, s), (1, s[:, ::-1, :])):
                    for w in range(NWIN):
                        t = tab[:, a, r, w, :].rearrange("p (r d) -> p r d", r=2)
                        dve.tensor_tensor(t, t, view, ALU.mult).then_inc(tab_made, 1)
            dve.wait_ge(tab_made, 4 * NWIN)
            dve.wait_ge(const_made, 12)

            def body(i):
                dve_steps.start(dve, i)
                step = dve_steps.step

                def wait_full(what):
                    name, n, k = FILL_AT[what]
                    dve.wait_ge(full[name].sem, full[name].at(i, k + 1))
                    return bank[name], read[name].sem

                def sum_squares(w):
                    dve.wait_ge(squared.sem, squared.at(i, w + 1))
                    step(dve.reduce_sum(sums[:, w, :], sq[:, :, :], AX.X))
                    dve.tensor_scalar(sums[:, w, :], sums[:, w, :], NORM_MIN ** 2, None, ALU.max)\
                       .then_inc(summed.sem, 1)

                def rotation_products(w):
                    _, n, _ = FILL_AT[("qk", w)]
                    dve.wait_ge(read["qk"].sem, read["qk"].at(i, n + 1))
                    name, _, k = FILL_AT[("kT", w - 1)] if w else FILL_AT[("fT", 1, 1)]
                    dve.wait_ge(full[name].sem, full[name].at(i, k + 1))
                    cos = tab[:, :, 0, w, :].unsqueeze(2).broadcast_to([P, 2, H2, D2])
                    dve.tensor_tensor(qk_rot[:, :, :, :], qk[:, :, :, :], cos, ALU.mult)
                    for a in range(2):
                        x = qk[:, a, :, :].rearrange("p h (r d) -> p h r d", r=2)[:, :, ::-1, :]
                        sin = tab[:, a, 1, w, :].rearrange("p (r d) -> p r d", r=2).unsqueeze(1)\
                            .broadcast_to([P, H2, 2, D2 // 2])
                        ins = dve.tensor_tensor(rot[:, a, :, :].rearrange("p h (r d) -> p h r d", r=2), x, sin,
                                                ALU.mult)
                    ins.then_inc(turned_parts.sem, 1)

                def finish_inverse(w):
                    dve.wait_ge(inv_near.sem, inv_near.at(i, w + 1))
                    newton_rsqrt(dve, dve_steps, inv[:, w, :], sums[:, w, :], inv_tmp[:, :]).then_inc(inv_done.sem, 1)
                    dve.wait_ge(inv_done.sem, inv_done.at(i, w + 1))
                    step(dve.tensor_scalar(scale_q[:, w, :], inv[:, w, 0:H2], QK_SCALE, None, ALU.mult))

                def take_qk(w):
                    src, back = wait_full(("qT", w))
                    dve.tensor_copy(q_t[:, :, :].rearrange("p a t -> p (a t)"), src[:, :]).then_inc(back, 1)
                    src, back = wait_full(("kT", w))
                    for hh in range(2):
                        rows = slice(D2 * hh, D2 * (hh + 1))
                        ins = dve.tensor_copy(k_t[rows, w % 2, hh:H2:2, :],
                                              src[rows, :].rearrange("p (a t) -> p a t", a=PAIRS))
                    ins.then_inc(back, 1)

                def row_tops(pp):
                    w, p = pp // PAIRS, pp % PAIRS
                    src, _ = wait_full(("s", pp))
                    lo = WIN if w == 0 else 0
                    step(dve.reduce_max(top[:, pp, :], src[:, :].rearrange("p (h s) -> p h s", h=2)[:, :, lo:], AX.X))
                    dve.scalar_tensor_tensor(out=bias[:, pp, :], in0=top[:, pp, :], scalar=-1.0,
                                             in1=scale_q[:, w, 2 * p:2 * p + 2], op0=ALU.mult, op1=ALU.mult)\
                       .then_inc(bias_done.sem, 1)

                def shares(pp):
                    name, n, _ = FILL_AT[("s", pp)]
                    dve.wait_ge(read[name].sem, read[name].at(i, n + 1))
                    dve.reciprocal(share[:, pp, :], total[:, pp, :]).then_inc(share_done.sem, 1)

                def take_turned(pp):
                    src, back = wait_full(("et", pp))
                    if pp >= 2:
                        dve.wait_ge(pairs_met.sem, pairs_met.at(i, pp - 1))
                    lo = 1 if pp < PAIRS else 0
                    dve.tensor_copy(e_t[:, pp % 2, :, :].rearrange("p (h b) t -> p h b t", h=2)[:, :, lo:, :],
                                    src[:, :].rearrange("p (h b t) -> p h b t", h=2, b=2)[:, :, lo:, :])\
                        .then_inc(back, 1)

                for n in range(4):
                    half, c = n // 2, n % 2
                    dve.wait_ge(f_hi.sem, f_hi.at(i, n + 1))
                    name, _, _ = FILL_AT[("fT", half, c)]
                    cols = slice(1 + 512 * half, 513 + 512 * half)
                    dve.tensor_tensor(turned[1][:, c, cols], bank[name][:, :], turned[0][:, c, cols].bitcast(F32),
                                      ALU.subtract).then_inc(read[name].sem, 1)
                sum_squares(0)
                rotation_products(0)
                finish_inverse(0)
                for pp in range(NPP + DRAIN):
                    w = pp // PAIRS
                    if pp % PAIRS == 0 and pp < NPP:
                        take_qk(w)
                    if pp < NPP:
                        row_tops(pp)
                    if w + 1 < NWIN and pp % PAIRS == 0:
                        sum_squares(w + 1)
                    if w + 1 < NWIN and pp % PAIRS == 1:
                        rotation_products(w + 1)
                    if w + 1 < NWIN and pp % PAIRS == 2:
                        finish_inverse(w + 1)
                    if 0 <= pp - 1 < NPP:
                        shares(pp - 1)
                    if 0 <= pp - 2 < NPP and pp % 2:
                        take_turned(pp - 2)
                    if 0 <= pp - 3 < NPP and (pp - 3) % PAIRS == PAIRS - 1:
                        done_w = (pp - 3) // PAIRS
                        dve.wait_ge(o_hi.sem, o_hi.at(i, done_w + 1))
                        dve.tensor_tensor(o_p[1][:, :, :].rearrange("p a t -> p (a t)"), bank["ot"][:, :],
                                          o_p[0][:, :, :].rearrange("p a t -> p (a t)").bitcast(F32), ALU.subtract)\
                            .then_inc(read["ot"].sem, 1)
                    if 0 <= pp - 4 < NPP and (pp - 4) % PAIRS == PAIRS - 1:
                        done_w = (pp - 4) // PAIRS
                        src, back = wait_full(("wo", done_w))
                        if done_w == 0:
                            dve.wait_ge(f_stored.sem, f_stored.at(i, 0))
                        dve.tensor_tensor(fr[:, done_w, :], src[:, 0:C], fl[:, done_w, :], ALU.add).then_inc(back, 1)

                _, n, _ = FILL_AT[("wo", NWIN - 1)]
                dve.wait_ge(read["t"].sem, read["t"].at(i, n + 1))
                for t in range(TB):
                    dve.bn_stats(stats[:, t, 0, :], fr[:, t, 0:P])
                dve.wait_ge(shifted.sem, shifted.at(i, 2 * NWIN - 1))
                for t in range(TB):
                    ins = dve.bn_stats(stats[:, t, 1, :], hs[:, t, :])
                step(ins)
                dve.memset(var_tmp[:, 0:1], 0.0)
                for t in range(TB):
                    ins = dve.bn_aggr(aggr[:, t, :], stats[:, t, :, :].rearrange("p a s -> p (a s)"))
                step(ins)
                dve.tensor_scalar(var[:, :], aggr[:, :, 1], LN_EPS, None, ALU.add).then_inc(moments.sem, 1)
                dve.wait_ge(rstd_near.sem, rstd_near.at(i, 1))
                step(newton_rsqrt(dve, dve_steps, rstd[:, :], var[:, :], var_tmp[:, :]))
                for t in range(TB):
                    for src, cols in ((fr[:, t, 0:P], slice(0, P)), (hs[:, t, :], slice(P, C))):
                        ins = dve.tensor_scalar(hn[:, t, cols], src, aggr[:, t, 0:1], rstd[:, t:t + 1],
                                                ALU.subtract, ALU.mult)
                ins.then_inc(normed.sem, 1)
                for n in range(4):
                    half, c = n // 2, n % 2
                    src, back = wait_full(("hT", half, c))
                    if n >= 2:
                        dve.wait_ge(h_lo.sem, h_lo.at(i, n - 1))
                    dve.tensor_scalar(wide[:, n % 2, :], src[:, :], ln_g[:, c:c + 1], ln_b[:, c:c + 1],
                                      ALU.mult, ALU.add).then_inc(back, 1)
                for n in range(2 * HK):
                    half, m = n // HK, n % HK
                    if m % 2:
                        name, k, _ = FILL_AT[("g", half, m)]
                        dve.wait_ge(read[name].sem, read[name].at(i, k + 1))
                    else:
                        dve.wait_ge(gelu_done.sem, gelu_done.at(i, n // 2 + 1))
                    if n < 2:
                        dve.wait_ge(h_lo.sem, h_lo.at(i, 3 + n))
                    else:
                        dve.wait_ge(hid_lo.sem, hid_lo.at(i, n - 1))
                    what = ("a" if m % 2 else "ag", half, m)
                    src, back = wait_full(what)
                    dve.scalar_tensor_tensor(out=wide[:, n % 2, :], in0=src[:, 0:512], scalar=b1_c[:, 0, m:m + 1],
                                             in1=gelu[:, n % 2, :], op0=ALU.add, op1=ALU.mult).then_inc(back, 1)
                    name, k, _ = FILL_AT[what]
                    dve.wait_ge(back, read[name].at(i, k + 1))
                    dve.tensor_copy(hid_p[0][:, m, :], wide[:, n % 2, :]).then_inc(hid_hi.sem, 1)
                    if m == HK - 1:
                        for t in range(4):
                            src, back = wait_full(("w2", 4 * half + t))
                            dve.wait_ge(b2_added.sem, b2_added.at(i, 1))
                            dve.tensor_tensor(fr[:, 4 * half + t, :], src[:, 0:C], fr[:, 4 * half + t, :], ALU.add)\
                               .then_inc(back, 1)
                dve_steps.end()

            loop(dve, body)



_INS = (["L0_attn_x", "L0_c", "L0_wmod"] + ["L0_attn_W" + n for n in "qkvp"] + ["L0_attn_b" + n for n in "qkvp"]
        + ["L0_ffn_" + n for n in ("wqkv", "q_scale", "k_scale", "wo", "ln_g", "ln_b", "w1", "b1", "w2", "b2")])
DEPTH = 2


def stage(nc, program, *args):
    with ExitStack() as ctx:
        sems = Semaphores(nc, ctx)
        program(nc, sems, *args)
        clear(nc, sems.all)


def build(nc, ins, tables, out, turns=B):
    scratch = lambda name, shape, dt=F32: nc.dram_tensor(name, shape, dt, kind="Internal").ap()
    mod = scratch("mod_rows", (B, NMOD, C))
    x1 = scratch("x1_rows", (B, T, C))
    f = [scratch(f"f_rows{n}", (B, T, C)) for n in range(DEPTH)]
    parts = [scratch(f"parts_{n}", (3, C, T), BF16) for n in "qk"]
    maxima = scratch("maxima", (G1, 3, 4 * T), BF16)
    stage(nc, modulation_stage, ins["L0_c"], ins["L0_wmod"], mod)
    stage(nc, attention_stage, ins["L0_attn_x"], [ins["L0_attn_W" + n] for n in "qkvp"],
                    [ins["L0_attn_b" + n] for n in "qkvp"], mod, x1, f[0], parts, maxima, turns)
    for layer in range(DEPTH):
        w = {n: ins["L0_ffn_" + n][layer] for n in ("wqkv", "q_scale", "k_scale", "wo", "ln_g", "ln_b", "w1", "b1",
                                                    "w2", "b2")}
        final = layer == DEPTH - 1
        stage(nc, layer_stage, f"b{layer}", f[layer], out if final else f[layer + 1], tables, w["wqkv"], w["q_scale"],
                    w["k_scale"], w["wo"], w["ln_g"], w["ln_b"], w["w1"], w["b1"], w["w2"], w["b2"], mod, x1, turns,
                    final)


def kernel(**inputs):
    import concourse.bacc as _bacc
    from concourse.bass_utils import run_bass_kernel_spmd as _run

    nc = _bacc.Bacc("TRN2", target_bir_lowering=False, num_devices=1)
    arrays, ins = {}, {}
    for name in _INS:
        arrays[f"in_{name}"] = np.ascontiguousarray(inputs[name])
        ins[name] = nc.dram_tensor(f"in_{name}", arrays[f"in_{name}"].shape, F32, kind="ExternalInput").ap()
    arrays["rotary_tables"] = rotary_tables()
    tables = nc.dram_tensor("rotary_tables", (4, T, D2), F32, kind="ExternalInput").ap()
    out = nc.dram_tensor("out_0", (B, T, C), F32, kind="ExternalOutput").ap()
    build(nc, ins, tables, out)
    r = _run(nc, [arrays], core_ids=[0])
    return r.results[0]["out_0"]
```

```python
from contextlib import ExitStack

import numpy as np

import concourse.bass as bass
from concourse import mybir

F32 = mybir.dt.float32
F32R = mybir.dt.float32r
BF16 = mybir.dt.bfloat16
I32 = mybir.dt.int32
ALU = mybir.AluOpType
ACT = mybir.ActivationFunctionType
AX = mybir.AxisListType

P = 128
B, T, C = 8, 1024, 256
TB = T // P
CK = C // P
NMOD = 6
LN_EPS = 1e-5
MASKED = -1e30

H1, D1 = 16, C // 16
G1 = H1 // 4
TERMS_Q = (0, 0, 1, 1, 0, 2)
TERMS_K = (0, 1, 0, 1, 2, 0)
KROWS = len(TERMS_Q) * D1
MROWS = KROWS + 3
VW = 32


def clear(nc, sems):
    with nc.Block() as block:
        @block.gpsimd
        def _(pool):
            for s in sems:
                pool.sem_clear(s)


class Semaphores:

    def __init__(self, nc, ctx):
        self.nc, self.ctx, self.all, self.signals = nc, ctx, [], []

    def enter_context(self, s):
        self.all.append(self.ctx.enter_context(s))
        return self.all[-1]


def prime(nc, signals):
    with nc.Block() as block:
        @block.gpsimd
        def _(pool):
            for s in signals:
                pool.sem_inc(s.sem, s.at(0, 0))


class Signal:

    def __init__(self, sems, nc, name, per, by=1):
        self.sem, self.per, self.by, self.seen = sems.enter_context(nc.semaphore(name)), per, by, 0
        sems.signals.append(self)

    def at(self, i, n):
        return i * (self.per * self.by) + ((self.per + n) * self.by + 1)

    def before(self, i, n):
        return self.at(i, n - self.per)


class Chain(Signal):

    def start(self, eng, i):
        self.eng, self.i, self.seen = eng, i, 0

    def step(self, ins):
        self.seen += 1
        ins.then_inc(self.sem, 1)
        self.eng.wait_ge(self.sem, self.at(self.i, self.seen))

    def end(self):
        assert self.seen == self.per, (self.seen, self.per)


def seed_rsqrt(eng, chain, y, v):
    bits_y, bits_v = y.bitcast(I32), v.bitcast(I32)
    chain.step(eng.tensor_scalar(bits_y, bits_v, 1, None, ALU.logical_shift_right))
    chain.step(eng.tensor_scalar(bits_y, bits_y, -1, 0x5f3759df, ALU.mult, ALU.add))


def newton_rsqrt(eng, chain, y, v, tmp):
    chain.step(eng.tensor_tensor(tmp, y, y, ALU.mult))
    chain.step(eng.scalar_tensor_tensor(out=tmp, in0=tmp, scalar=-0.5, in1=v, op0=ALU.mult, op1=ALU.mult))
    return eng.scalar_tensor_tensor(out=y, in0=tmp, scalar=1.5, in1=y, op0=ALU.add, op1=ALU.mult)


def modulation_stage(nc, sems, c_in, wmod, mod_dram):
    with ExitStack() as ctx:
        sb = lambda name, shape, dt=F32: ctx.enter_context(nc.sbuf_tensor(name, shape, dt))
        ps = lambda name, shape, dt=F32: ctx.enter_context(nc.psum_tensor(name, shape, dt))
        cond = sb("m_cond", [B, C])
        grown = sb("m_grown", [B, C])
        silu = sb("m_silu", [B, C])
        silu_t = sb("m_silu_t", [P, CK, B])
        w = sb("m_w", [P, CK, NMOD * C])
        mod = sb("m_mod", [B, NMOD, C])
        size = sb("m_size", [B, 2, C])
        sign = sb("m_sign", [B, 2, C])
        ident = sb("m_ident", [B, B])
        pt = ps("m_pt", [P, CK, B])
        pm = ps("m_pm", [B, NMOD // 2, 2 * C])
        loaded = sems.enter_context(nc.semaphore("m_loaded"))
        w_loaded = sems.enter_context(nc.semaphore("m_w_loaded"))
        ident_made = sems.enter_context(nc.semaphore("m_ident_made"))
        exp_done = sems.enter_context(nc.semaphore("m_exp_done"))
        turned = sems.enter_context(nc.semaphore("m_turned"))
        silu_done = sems.enter_context(nc.semaphore("m_silu_done"))
        silu_t_done = sems.enter_context(nc.semaphore("m_silu_t_done"))
        product = sems.enter_context(nc.semaphore("m_product"))
        rows_done = sems.enter_context(nc.semaphore("m_rows_done"))
        stored = sems.enter_context(nc.semaphore("m_stored"))
        steps = Chain(sems, nc, "m_steps", 9)
        prime(nc, sems.signals)
        block = ctx.enter_context(nc.Block())

        @block.sync
        def _(sp):
            sp.dma_start(cond[:, :], c_in).then_inc(loaded, 16)
            sp.dma_start(w[:, :, :], wmod.rearrange("(k p) n -> p k n", p=P)).then_inc(w_loaded, 16)
            sp.wait_ge(rows_done, 1)
            sp.dma_start(mod_dram, mod[:, :, :]).then_inc(stored, 16)
            sp.wait_ge(stored, 16)

        @block.gpsimd
        def _(pool):
            pool.memset(ident[:, :], 0.0).then_inc(ident_made, 1)
            pool.wait_ge(ident_made, 1)
            pool.affine_select(out=ident[:, :], in_=ident[:, :], compare_op=ALU.not_equal, fill=1.0,
                               base=0, pattern=[[-1, B]], channel_multiplier=1).then_inc(ident_made, 1)

        @block.scalar
        def _(act):
            act.wait_ge(loaded, 16)
            act.activation(grown[:, :], cond[:, :], ACT.Exp, scale=-1.0).then_inc(exp_done, 1)

        @block.tensor
        def _(pe):
            pe.wait_ge(ident_made, 2)
            pe.wait_ge(silu_done, 1)
            for k in range(CK):
                mm = pe.transpose(pt[:, k, :], silu[:, k * P:(k + 1) * P], ident[:, :])
            mm.then_inc(turned, 1)
            pe.wait_ge(silu_t_done, 1)
            pe.wait_ge(w_loaded, 16)
            for j in range(NMOD // 2):
                for k in range(CK):
                    mm = pe.matmul(pm[:, j, :], silu_t[:, k, :], w[:, k, j * 2 * C:(j + 1) * 2 * C],
                                   start=(k == 0), stop=(k == CK - 1))
            mm.then_inc(product, 1)

        @block.vector
        def _(dve):
            steps.start(dve, 0)
            dve.wait_ge(exp_done, 1)
            steps.step(dve.tensor_scalar(grown[:, :], grown[:, :], 1.0, None, ALU.add))
            steps.step(dve.reciprocal(grown[:, :], grown[:, :]))
            dve.tensor_tensor(silu[:, :], cond[:, :], grown[:, :], ALU.mult).then_inc(silu_done, 1)
            dve.wait_ge(turned, 1)
            dve.tensor_copy(silu_t[:, :, :], pt[:, :, :]).then_inc(silu_t_done, 1)
            dve.wait_ge(product, 1)
            raw = pm[:, :, :].rearrange("b j (r c) -> b (j r) c", r=2)
            steps.step(dve.tensor_copy(mod[:, :, :], raw))
            scales, gates = mod[:, 1:5:3, :], mod[:, 2:6:3, :]
            steps.step(dve.tensor_scalar(scales, scales, 1.0, None, ALU.add))
            steps.step(dve.scalar_tensor_tensor(out=size[:, :, :], in0=gates, scalar=-1.0, in1=gates,
                                                op0=ALU.mult, op1=ALU.max))
            steps.step(dve.tensor_scalar(size[:, :, :], size[:, :, :], 0.25, None, ALU.max))
            steps.step(dve.tensor_scalar(sign[:, :, :], gates, 0.0, 2.0, ALU.is_ge, ALU.mult))
            steps.step(dve.tensor_scalar(sign[:, :, :], sign[:, :, :], 1.0, None, ALU.subtract))
            steps.step(dve.tensor_tensor(gates, size[:, :, :], sign[:, :, :], ALU.mult))
            steps.end()
            dve.tensor_copy(cond[:, 0:1], mod[:, 0, 0:1]).then_inc(rows_done, 1)


def score_steps():
    return [(half, s) for half in range(2) for s in range(4 * half + 4)]


STEPS1 = score_steps()
NSTEP = len(STEPS1)
RING_FILLS = ([("s2", g, n, pair) for g in range(G1) for n in range(NSTEP) for pair in range(2)]
              + [("yT", c) for c in range(CK)] + [("wp", p) for p in range(2)])
RING_AT = {fill: n for n, fill in enumerate(RING_FILLS)}
MATRICES = (0, CK, 1, CK + 1)
PREP_FILLS = [("xT", c) for c in range(CK)] + [("qk", m) for m in MATRICES] + [("v", p) for p in range(2)]
PREP_AT = {fill: n for n, fill in enumerate(PREP_FILLS)}
assert len(RING_FILLS) % 2 == 0 and len(PREP_FILLS) % 2 == 0
LAST = G1 - 1

UNITS = [(h, t, piece) for t in range(TB) for h in range(4) for piece in range(t // 4 + 1)]
NUNIT = len(UNITS)
PAIRED = TB // 2
UNIT_COLS = PAIRED + 2 * (TB - PAIRED)
def unit_col(t, piece):
    return t if t < PAIRED else PAIRED + 2 * (t - PAIRED) + piece


PASS1_AT = {1: (2, 5, 11), 2: (0, 4, 11), 3: (0, 5, 10), 0: (3, 6, 11)}


def units_in(g, n):
    start, rate, _ = PASS1_AT[g]
    n = max(n - start, -1) if n >= start else -1
    return range(min(NUNIT, rate * n), min(NUNIT, rate * (n + 1))) if n >= 0 else range(0)


AT_COPY0, AT_TURN0, AT_COPY1, AT_TURN1 = 4, 6, 0, 1


def attention_stage(nc, sems, x_in, w_in, b_in, mod_dram, x1_dram, f_dram, parts_dram, max_dram, turns):
    with ExitStack() as ctx:
        sb = lambda name, shape, dt=F32: ctx.enter_context(nc.sbuf_tensor(name, shape, dt))
        ps = lambda name, shape, dt=F32: ctx.enter_context(nc.psum_tensor(name, shape, dt))
        sig = lambda name, per, by=1: Signal(sems, nc, name, per, by)
        plain = lambda name: sems.enter_context(nc.semaphore(name))

        NW = 4
        w_hi = sb("a_w_hi", [P, CK, NW, C], F32R)
        w_lo = sb("a_w_lo", [P, CK, NW, C], F32R)
        b_qk = sb("a_b_qk", [P, 2, CK])
        b_v = sb("a_b_v", [P, C])
        b_p = sb("a_b_p", [P, C])
        gate_bp = sb("a_gate_bp", [P, 1, C])
        ident = sb("a_ident", [P, P])
        ident_bf = sb("a_ident_bf", [P, P], BF16)
        mask_ts = sb("a_mask_ts", [P, P], BF16)
        mask_st = sb("a_mask_st", [P, P], BF16)
        mod_in = sb("a_mod_in", [P, 2, C])
        modb = sb("a_modb", [P, NMOD - 3, C])
        xl = sb("a_xl", [P, TB, C])
        x1 = sb("a_x1", [P, TB, C])
        stats = sb("a_stats", [P, TB, 6])
        aggr = sb("a_aggr", [P, TB, 2])
        rstd = sb("a_rstd", [P, TB])
        var = sb("a_var", [P, TB])
        var_tmp = sb("a_var_tmp", [P, TB])
        h_hi = sb("a_h_hi", [P, CK, T], F32R)
        h_lo = sb("a_h_lo", [P, CK, T], F32R)
        qk = sb("a_qk", [P, 2 * CK, T])
        qk_part = sb("a_qk_part", [P, 2, 3, T], BF16)
        q_st = sb("a_q_st", [MROWS, H1, T], BF16)
        k_st = sb("a_k_st", [MROWS, H1, T], BF16)
        v_t = sb("a_v_t", [P, TB, H1, VW])
        e_t = sb("a_e_t", [P, 2, 4, 512])
        w_raw = e_t[:, :, :, :].rearrange("p a b (c n) -> p (a b c) n", n=C)[:, 0:CK * NW, :]\
            .rearrange("p (k w) n -> p k w n", k=CK)
        mx = sb("a_mx", [P, 4, UNIT_COLS])
        mx_neg = sb("a_mx_neg", [P, 4, UNIT_COLS])
        nm = sb("a_nm", [P, 4, TB])
        m_rest = sb("a_m_rest", [4 * TB, P])
        m_part = sb("a_m_part", [4 * TB, 3, P], BF16)
        o_un = sb("a_o_un", [P, 512])
        o_rec = sb("a_o_rec", [P, 4, 4])
        y = sb("a_y", [P, TB, C])

        ring = [ps(f"a_ring{n}", [P, 1024]) for n in range(2)]
        unit = [ps(f"a_unit{n}", [P, 512]) for n in range(2)]
        outp = ps("a_outp", [P, 512])
        misc = ps("a_misc", [P, 512])

        NR, NU, NPREP = len(RING_FILLS), LAST * NUNIT, len(PREP_FILLS)
        NT = len(TERMS_Q)
        w_loaded = plain("a_w_loaded")
        const_made = plain("a_const_made")
        hi_split = plain("a_w_hi_split")
        lo_split = plain("a_w_lo_split")
        x_loaded = sig("a_x_loaded", 1, 16)
        mod_in_loaded = sig("a_mod_in_loaded", 1, 16)
        x_normed = sig("a_x_normed", 1)
        x_scaled = sig("a_x_scaled", 1)
        h_ready = sig("a_h_ready", 1)
        prep_full = [sig(f"a_prep_full{n}", NPREP // 2) for n in range(2)]
        prep_read = [sig(f"a_prep_read{n}", NPREP // 2) for n in range(2)]
        xT_hi = sig("a_xT_hi", CK)
        part0_done = sig("a_part0_done", 2 * CK)
        rest_done = sig("a_rest_done", 2 * CK)
        part1_done = sig("a_part1_done", 2 * CK)
        qk_split = sig("a_qk_split", 2 * CK)
        parts_stored = [sig(f"a_parts_stored{n}", CK, 16) for n in range(2)]
        stacks_loaded = [sig(f"a_stacks_loaded{g}", 2 * NT, 16) for g in range(G1)]
        unit0_full = [sig(f"a_unit0_full{n}", NUNIT // 2) for n in range(2)]
        unit0_read = [sig(f"a_unit0_read{n}", NUNIT // 2) for n in range(2)]
        nm_done = [sig(f"a_nm_done{g}", 1) for g in range(G1)]
        max_turned = [sig(f"a_max_turned{g}", 1) for g in range(G1)]
        max_taken = [sig(f"a_max_taken{g}", 1) for g in range(G1)]
        max_split = [sig(f"a_max_split{g}", 1) for g in range(G1)]
        max_stored = [sig(f"a_max_stored{g}", 1, 16) for g in range(G1)]
        max_loaded = [sig(f"a_max_loaded{g}", 1, 16) for g in range(G1)]
        mod_loaded = sig("a_mod_loaded", 1, 16)
        xr_loaded = sig("a_xr_loaded", 1, 16)
        ring_full = [sig(f"a_ring_full{n}", NR // 2) for n in range(2)]
        ring_read = [sig(f"a_ring_read{n}", NR // 2) for n in range(2)]
        unit_full = [sig(f"a_unit_full{n}", NU // 2) for n in range(2)]
        unit_read = [sig(f"a_unit_read{n}", NU // 2) for n in range(2)]
        out_turned = sig("a_out_turned", 2 * G1)
        out_taken = sig("a_out_taken", 2 * G1)
        out_read = sig("a_out_read", 2 * G1)
        yT_hi = sig("a_yT_hi", CK)
        values_met = sig("a_values_met", G1 * NSTEP)
        biased = sig("a_biased", 1)
        x1_done = sig("a_x1_done", 2)
        x1_normed = sig("a_x1_normed", 1)
        f_done = sig("a_f_done", 1)
        x1_stored = sig("a_x1_stored", 1, 16)
        f_stored = sig("a_f_stored", 1, 16)
        NORM_STEPS, MAXIMA_STEPS = 14, 5
        lead_steps = Chain(sems, nc, "a_lead_steps", NORM_STEPS + MAXIMA_STEPS)
        dve_steps = Chain(sems, nc, "a_dve_steps", 2 * NORM_STEPS + G1 * MAXIMA_STEPS + 2 * G1)
        pool_steps = Chain(sems, nc, "a_pool_steps", 2)
        prime(nc, sems.signals)
        block = ctx.enter_context(nc.Block())

        def ring_slot(fill):
            at, full, read = ((PREP_AT, prep_full, prep_read) if fill in PREP_AT else (RING_AT, ring_full, ring_read))
            n = at[fill]
            return ring[n % 2], full[n % 2], read[n % 2], n // 2

        def unit_slot(g, u):
            n = u if g == 0 else (g - 1) * NUNIT + u
            full, read = (unit0_full, unit0_read) if g == 0 else (unit_full, unit_read)
            return unit[n % 2], full[n % 2], read[n % 2], n // 2

        def loop(eng, body):
            if turns == 1:
                body(0)
            else:
                with eng.Fori(0, turns) as i:
                    body(i)

        rows_of = lambda dram, i: dram[i].rearrange("(t p) c -> p t c", p=P)
        mod_rows = lambda i, lo, hi: mod_dram[i, lo:hi, :].rearrange("r c -> (r c)").partition_broadcast(P)

        @block.sync
        def _(sp):
            sp.dma_start(xl[:, :, :], rows_of(x_in, 0)).then_inc(x_loaded.sem, 16)
            sp.dma_start(mod_in[:, :, :].rearrange("p r c -> p (r c)"), mod_rows(0, 0, 2)).then_inc(mod_in_loaded.sem, 16)
            for n in range(NW):
                sp.dma_start(w_raw[:, :, n, :], w_in[n].rearrange("(k p) n -> p k n", p=P)).then_inc(w_loaded, 16)
            with nc.allow_non_contiguous_dma(reason="the biases of q and k go one to a partition"):
                for n in range(2):
                    sp.dma_start(b_qk[:, n, :], b_in[n].rearrange("(m p) -> p m", p=P)).then_inc(w_loaded, 16)
            sp.dma_start(b_v[:, :], b_in[2].partition_broadcast(P)).then_inc(w_loaded, 16)
            sp.dma_start(b_p[:, :], b_in[3].partition_broadcast(P)).then_inc(w_loaded, 16)

            def store_parts(j, ahead):
                m, stored = MATRICES[j], parts_stored[j % 2]
                sp.wait_ge(qk_split.sem, qk_split.at(ahead, j + 1))
                sp.dma_start(parts_dram[m // CK][:, (m % CK) * P:(m % CK + 1) * P, :].rearrange("j p t -> p j t"),
                             qk_part[:, j % 2, :, :]).then_inc(stored.sem, 16)

            def load_stacks(g, ahead):
                for n in range(2):
                    sp.wait_ge(parts_stored[n].sem, parts_stored[n].at(ahead, 1 + g // (G1 // CK)))
                for st, terms, w in ((q_st, TERMS_Q, 0), (k_st, TERMS_K, 1)):
                    for j, part in enumerate(terms):
                        sp.dma_start(st[j * D1:(j + 1) * D1, 4 * g:4 * g + 4, :],
                                     parts_dram[w][part, 4 * g * D1:(4 * g + 4) * D1, :]
                                     .rearrange("(h d) t -> d h t", d=D1)).then_inc(stacks_loaded[g].sem, 16)

            def pass_maxima(g, i):
                sp.wait_ge(max_split[g].sem, max_split[g].at(i, 1))
                sp.dma_start(max_dram[g].rearrange("j (r t) -> r j t", t=P), m_part[:, :, :])\
                  .then_inc(max_stored[g].sem, 16)
                sp.wait_ge(max_stored[g].sem, max_stored[g].at(i, 1))
                sp.dma_start(q_st[KROWS:MROWS, 4 * g:4 * g + 4, :],
                             max_dram[g].rearrange("j (h t) -> j h t", t=T)).then_inc(max_loaded[g].sem, 16)

            for j in range(2 * CK):
                store_parts(j, 0)
            for g in range(G1):
                load_stacks(g, 0)
            pass_maxima(0, 0)

            def body(i):
                nxt = 0 if turns == 1 else (i + 1) % turns
                sp.wait_ge(f_done.sem, f_done.at(i, 0))
                sp.dma_start(modb[:, :, :].rearrange("p r c -> p (r c)"), mod_rows(i, 2, NMOD - 1))\
                  .then_inc(mod_loaded.sem, 16)
                sp.dma_start(xl[:, :, :], rows_of(x_in, nxt)).then_inc(x_loaded.sem, 16)
                sp.dma_start(mod_in[:, :, :].rearrange("p r c -> p (r c)"), mod_rows(nxt, 0, 2))\
                  .then_inc(mod_in_loaded.sem, 16)
                sp.wait_ge(x1_stored.sem, x1_stored.at(i, 0))
                sp.dma_start(x1[:, :, :], rows_of(x_in, i)).then_inc(xr_loaded.sem, 16)
                pass_maxima(1, i)
                pass_maxima(2, i)
                store_parts(0, i + 1)
                store_parts(1, i + 1)
                load_stacks(0, i + 1)
                load_stacks(1, i + 1)
                store_parts(2, i + 1)
                store_parts(3, i + 1)
                pass_maxima(3, i)
                pass_maxima(0, i + 1)
                load_stacks(2, i + 1)
                load_stacks(LAST, i + 1)
                sp.wait_ge(x1_done.sem, x1_done.at(i, 2))
                sp.dma_start(rows_of(x1_dram, i), x1[:, :, :]).then_inc(x1_stored.sem, 16)
                sp.wait_ge(f_done.sem, f_done.at(i, 1))
                sp.dma_start(rows_of(f_dram, i), y[:, :, :]).then_inc(f_stored.sem, 16)

            loop(sp, body)
            sp.wait_ge(f_stored.sem, f_stored.at(turns, 0))
            sp.wait_ge(x1_stored.sem, x1_stored.at(turns, 0))
            sp.wait_ge(x_loaded.sem, x_loaded.at(turns, 1))
            sp.wait_ge(mod_in_loaded.sem, mod_in_loaded.at(turns, 1))
            sp.wait_ge(max_loaded[0].sem, max_loaded[0].at(turns, 1))
            for g in range(G1):
                sp.wait_ge(stacks_loaded[g].sem, stacks_loaded[g].at(turns, 2 * NT))

        @block.gpsimd
        def _(pool):
            pool.memset(ident[:, :], 0.0).then_inc(const_made, 1)
            pool.memset(ident_bf[:, :], 0.0).then_inc(const_made, 1)
            pool.memset(mask_ts[:, :], 0.0).then_inc(const_made, 1)
            pool.memset(mask_st[:, :], 0.0).then_inc(const_made, 1)
            pool.memset(v_t[:, :, :, D1:VW], 0.0).then_inc(const_made, 1)
            pool.wait_ge(const_made, 5)
            pool.memset(v_t[:, :, :, D1:D1 + 1], 1.0).then_inc(const_made, 1)
            pool.wait_ge(const_made, 6)
            pool.memset(k_st[KROWS:MROWS, :, :], 1.0).then_inc(const_made, 1)
            pool.wait_ge(const_made, 7)
            for m in (ident, ident_bf):
                pool.affine_select(out=m[:, :], in_=m[:, :], compare_op=ALU.not_equal, fill=1.0, base=0,
                                   pattern=[[-1, P]], channel_multiplier=1).then_inc(const_made, 1)
            pool.affine_select(out=mask_ts[:, :], in_=mask_ts[:, :], compare_op=ALU.is_ge, fill=MASKED, base=0,
                               pattern=[[-1, P]], channel_multiplier=1).then_inc(const_made, 1)
            pool.affine_select(out=mask_st[:, :], in_=mask_st[:, :], compare_op=ALU.is_ge, fill=MASKED, base=0,
                               pattern=[[1, P]], channel_multiplier=-1).then_inc(const_made, 1)
            pool.wait_ge(w_loaded, 16 * (NW + 4))

            def modulate_x(ahead):
                row = lambda r: mod_in[:, r:r + 1, :].broadcast_to([P, TB, C])
                pool.wait_ge(mod_in_loaded.sem, mod_in_loaded.at(ahead, 1))
                pool.wait_ge(x_normed.sem, x_normed.at(ahead, 1))
                pool.tensor_tensor(xl[:, :, :], xl[:, :, :], row(1), ALU.mult).then_inc(x_scaled.sem, 1)
                pool.wait_ge(x_scaled.sem, x_scaled.at(ahead, 1))
                pool.tensor_tensor(xl[:, :, :], xl[:, :, :], row(0), ALU.add).then_inc(h_ready.sem, 1)

            modulate_x(0)

            def body(i):
                pool_steps.start(pool, i)
                row = lambda r: modb[:, r - 2:r - 1, :].broadcast_to([P, TB, C])

                pool.wait_ge(mod_loaded.sem, mod_loaded.at(i, 1))
                pool.wait_ge(xr_loaded.sem, xr_loaded.at(i, 1))
                pool_steps.step(pool.tensor_tensor(gate_bp[:, 0, :], modb[:, 0, :], b_p[:, :], ALU.mult))
                pool.tensor_tensor(x1[:, :, :], x1[:, :, :], gate_bp[:, :, :].broadcast_to([P, TB, C]),
                                   ALU.add).then_inc(biased.sem, 1)
                pool.wait_ge(biased.sem, biased.at(i, 1))
                modulate_x(i + 1)
                for p in range(2):
                    _, _, read, k = ring_slot(("wp", p))
                    pool.wait_ge(read.sem, read.at(i, k + 1))
                    half = slice(4 * p, 4 * p + 4)
                    pool.tensor_tensor(x1[:, half, :], x1[:, half, :], xl[:, half, :], ALU.add)\
                        .then_inc(x1_done.sem, 1)
                pool.wait_ge(x1_normed.sem, x1_normed.at(i, 1))
                pool_steps.step(pool.tensor_tensor(y[:, :, :], y[:, :, :], row(4), ALU.mult))
                pool.tensor_tensor(y[:, :, :], y[:, :, :], row(3), ALU.add).then_inc(f_done.sem, 1)
                pool_steps.end()

            loop(pool, body)

        @block.scalar
        def _(act):
            act.wait_ge(w_loaded, 16 * (NW + 4))
            act.activation(w_hi[:, :, :, :], w_raw, ACT.Copy).then_inc(hi_split, 1)
            act.mul(b_qk[:, 0, :], b_qk[:, 0, :], D1 ** -0.5).then_inc(hi_split, 1)
            act.wait_ge(hi_split, 2)
            act.wait_ge(lo_split, 1)

            def high(what, done, i):
                for c in range(CK):
                    slot, full, _, k = ring_slot((what, c))
                    act.wait_ge(full.sem, full.at(i, k + 1))
                    act.activation(h_hi[:, c, :], slot[:, :], ACT.Copy).then_inc(done.sem, 1)

            def take_qk(ahead):
                for j, m in enumerate(MATRICES):
                    slot, full, read, k = ring_slot(("qk", m))
                    act.wait_ge(full.sem, full.at(ahead, k + 1))
                    act.activation(qk[:, j, :], slot[:, :], ACT.Identity, bias=b_qk[:, m // CK, m % CK:m % CK + 1],
                                   scale=D1 ** -0.5 if m < CK else 1.0).then_inc(read.sem, 1)

            def part0(j, ahead, before=None):
                _, _, read, k = ring_slot(("qk", MATRICES[j]))
                act.wait_ge(read.sem, read.at(ahead, k + 1))
                stored = parts_stored[j % 2]
                act.wait_ge(stored.sem, stored.at(ahead, j // 2))
                if j == 0 and before is not None:
                    act.wait_ge(stacks_loaded[LAST].sem, stacks_loaded[LAST].at(before, 2 * NT))
                act.activation(qk_part[:, j % 2, 0, :], qk[:, j, :], ACT.Copy).then_inc(part0_done.sem, 1)

            def part1(j, ahead):
                act.wait_ge(rest_done.sem, rest_done.at(ahead, j + 1))
                act.activation(qk_part[:, j % 2, 1, :], qk[:, j, :], ACT.Copy).then_inc(part1_done.sem, 1)

            high("xT", xT_hi, 0)
            take_qk(0)
            for j in range(2 * CK):
                part0(j, 0)
                part1(j, 0)

            def body(i):
                for g in range(G1):
                    if g == LAST - 1:
                        high("xT", xT_hi, i + 1)
                        take_qk(i + 1)
                    for n in range(NSTEP):
                        half, s = STEPS1[n]
                        step = g * NSTEP + n
                        for pair in range(2):
                            slot, full, read, k = ring_slot(("s2", g, n, pair))
                            act.wait_ge(full.sem, full.at(i, k + 1))
                            if pair == 0:
                                act.wait_ge(values_met.sem, values_met.at(i, max(step - 1, 0)))
                            cols = 512 * (half + 1) - max(512 * half, P * s)
                            act.activation(e_t[:, step % 2, 2 * pair:2 * pair + 2, 0:cols],
                                           slot[:, :].rearrange("p (h t) -> p h t", h=2)[:, :, 0:cols],
                                           ACT.Exp).then_inc(read.sem, 1)
                        if g == LAST - 1 and n < 4 * CK:
                            if n % 2 == 0:
                                part0(n // 2, i + 1, i)
                            else:
                                part1(n // 2, i + 1)
                high("yT", yT_hi, i)

            loop(act, body)

        @block.tensor
        def _(pe):
            pe.wait_ge(const_made, 11)
            pe.wait_ge(lo_split, 1)

            def program(i, ahead, lead=False):
                def when(what):
                    return ahead if what in PREP_AT else i

                def fill(what):
                    slot, full, read, k = ring_slot(what)
                    pe.wait_ge(read.sem, read.at(when(what), k))
                    return slot, full

                def ring_passes(*last):
                    for what in last:
                        if not lead or what in PREP_AT:
                            read_of(what)

                def read_of(what):
                    _, _, read, k = ring_slot(what)
                    pe.wait_ge(read.sem, read.at(when(what), k + 1))

                def turn_chunks(what, src):
                    for c in range(CK):
                        slot, full = fill((what, c))
                        for t in range(TB):
                            mm = pe.transpose(slot[:, t * P:(t + 1) * P], src[:, t, c * P:(c + 1) * P], ident[:, :])
                        mm.then_inc(full.sem, 1)

                def three(out, lhs, rhs, first, last):
                    for j, (a, b) in enumerate(((0, 0), (0, 1), (1, 0))):
                        mm = pe.matmul(out, lhs[a], rhs[b], start=(first and j == 0), stop=(last and j == 2))
                    return mm

                def project_tokens(what, w, p):
                    slot, full = fill((what, p))
                    for t in range(4):
                        tok = slice((4 * p + t) * P, (4 * p + t + 1) * P)
                        for c in range(CK):
                            mm = three(slot[:, t * C:(t + 1) * C], (h_hi[:, c, tok], h_lo[:, c, tok]),
                                       (w_hi[:, c, w, :], w_lo[:, c, w, :]), c == 0, c == CK - 1)
                    mm.then_inc(full.sem, 1)

                def project_qk():
                    pe.wait_ge(h_ready.sem, h_ready.at(ahead, 1))
                    turn_chunks("xT", xl)
                    for c in range(CK):
                        read_of(("xT", c))
                    for m in MATRICES:
                        slot, full = fill(("qk", m))
                        w, col = m // CK, slice((m % CK) * P, (m % CK + 1) * P)
                        for half in range(2):
                            tok = slice(512 * half, 512 * half + 512)
                            for c in range(CK):
                                mm = three(slot[:, tok], (w_hi[:, c, w, col], w_lo[:, c, w, col]),
                                           (h_hi[:, c, tok], h_lo[:, c, tok]), c == 0, c == CK - 1)
                        mm.then_inc(full.sem, 1)

                def first_pass(g, units):
                    for u in units:
                        h, t, piece = UNITS[u]
                        slot, full, read, k = unit_slot(g, u)
                        pe.wait_ge(read.sem, read.at(ahead if g == 0 else i, k))
                        if u == 0 and not lead:
                            for m in range(2):
                                if g == 0:
                                    pe.wait_ge(unit_read[m].sem, unit_read[m].at(i, NU // 2))
                                elif g == 1:
                                    pe.wait_ge(unit0_read[m].sem, unit0_read[m].at(i, NUNIT // 2))
                        head = 4 * g + h
                        cols = min(512, (t + 1) * P - 512 * piece)
                        diagonal = piece == t // 4
                        mm = pe.matmul(slot[:, 0:cols], q_st[0:KROWS, head, t * P:(t + 1) * P],
                                       k_st[0:KROWS, head, 512 * piece:512 * piece + cols],
                                       start=True, stop=not diagonal)
                        if diagonal:
                            mm = pe.matmul(slot[:, cols - P:cols], ident_bf[:, :], mask_ts[:, :],
                                           start=False, stop=True)
                        mm.then_inc(full.sem, 1)

                def turn_maxima(g):
                    k = ahead if g == 0 else i
                    pe.wait_ge(nm_done[g].sem, nm_done[g].at(k, 1))
                    if not lead:
                        pe.wait_ge(out_taken.sem, out_taken.at(i, 2 * ((g - 1) % G1) + 1))
                    pe.transpose(misc[0:4 * TB, 0:P], nm[:, :, :].rearrange("p h t -> p (h t)"), ident[:, :])\
                      .then_inc(max_turned[g].sem, 1)

                def scores(g, n, pair, beside):
                    half, s = STEPS1[n]
                    lo = max(512 * half, P * s)
                    cols = 512 * (half + 1) - lo
                    diagonal = P * s >= 512 * half
                    slot, full = fill(("s2", g, n, pair))
                    for hh in range(2):
                        head = 4 * g + 2 * pair + hh
                        mm = pe.matmul(slot[:, 512 * hh:512 * hh + cols], k_st[:, head, s * P:(s + 1) * P],
                                       q_st[:, head, lo:lo + cols], start=True, stop=not diagonal)
                        if diagonal:
                            mm = pe.matmul(slot[:, 512 * hh:512 * hh + P], ident_bf[:, :], mask_st[:, :],
                                           start=False, stop=True)
                        if hh == 0:
                            beside()
                    mm.then_inc(full.sem, 1)
                    beside()

                def meet_values(g, n, beside=lambda: None):
                    half, s = STEPS1[n]
                    lo = max(512 * half, P * s) - 512 * half
                    for pair in range(2):
                        read_of(("s2", g, n, pair))
                    if s == 0:
                        pe.wait_ge(out_read.sem, out_read.at(i, 2 * g + half))
                    for h in range(4):
                        mm = pe.matmul(outp[32 * h:32 * h + VW, lo:512], v_t[:, s, 4 * g + h, :],
                                       e_t[:, (g * NSTEP + n) % 2, h, 0:512 - lo],
                                       start=(s == 0), stop=(s == 4 * half + 3))
                        if h == 1:
                            beside()
                    mm.then_inc(values_met.sem, 1)
                    beside()

                def turn_output(g, half):
                    pe.wait_ge(out_read.sem, out_read.at(i, 2 * g + half + 1))
                    if half == 0:
                        pe.wait_ge(out_taken.sem, out_taken.at(i, 2 * g))
                    else:
                        nxt = (g + 1) % G1
                        pe.wait_ge(max_taken[nxt].sem, max_taken[nxt].at(ahead if nxt == 0 else i, 1))
                    for t in range(4):
                        mm = pe.transpose(misc[:, t * P:(t + 1) * P], o_un[:, t * P:(t + 1) * P], ident[:, :])
                    mm.then_inc(out_turned.sem, 1)

                if lead:
                    project_qk()
                    for p in range(2):
                        project_tokens("v", 2, p)
                    pe.wait_ge(stacks_loaded[0].sem, stacks_loaded[0].at(ahead, 2 * NT))
                    first_pass(0, range(NUNIT))
                    turn_maxima(0)
                    ring_passes(("v", 0), ("v", 1))
                    return
                for g in range(G1):
                    nxt = (g + 1) % G1
                    if g == LAST - 1:
                        ring_passes(("s2", g - 1, NSTEP - 1, 0), ("s2", g - 1, NSTEP - 1, 1))
                        project_qk()
                        ring_passes(("qk", MATRICES[-2]), ("qk", MATRICES[-1]))
                    pe.wait_ge(max_loaded[g].sem, max_loaded[g].at(i, 1))
                    for n in range(NSTEP):
                        units = units_in(nxt, n)
                        if len(units) and units[0] == 0:
                            pe.wait_ge(stacks_loaded[nxt].sem,
                                       stacks_loaded[nxt].at(ahead if nxt == 0 else i, 2 * NT))
                        left = list(units)
                        beside = lambda: first_pass(nxt, [left.pop(0)]) if left else None
                        scores(g, n, 0, beside)
                        scores(g, n, 1, beside)
                        if n > 0:
                            meet_values(g, n - 1, beside)
                        elif g > 0:
                            meet_values(g - 1, NSTEP - 1, beside)
                        first_pass(nxt, left)
                        if n == AT_TURN0:
                            turn_output(g, 0)
                        if n == AT_TURN1 and g > 0:
                            turn_output(g - 1, 1)
                        if n == PASS1_AT[nxt][2]:
                            turn_maxima(nxt)
                meet_values(LAST, NSTEP - 1)
                project_tokens("v", 2, 0)
                turn_output(LAST, 1)
                project_tokens("v", 2, 1)
                pe.wait_ge(out_taken.sem, out_taken.at(i, 2 * G1))
                ring_passes(("v", 0), ("v", 1))
                turn_chunks("yT", y)
                for c in range(CK):
                    read_of(("yT", c))
                for p in range(2):
                    project_tokens("wp", 3, p)

            program(None, 0, lead=True)

            def body(i):
                program(i, i + 1)

            loop(pe, body)

        @block.vector
        def _(dve):
            dve.wait_ge(hi_split, 1)
            dve.tensor_tensor(w_lo[:, :, :, :], w_raw, w_hi[:, :, :, :].bitcast(F32), ALU.subtract)\
                .then_inc(lo_split, 1)

            def program(i, ahead, chain, lead=False):
                chain.start(dve, 0 if lead else i)
                step = chain.step

                def statistics(src, ts):
                    for t in ts:
                        ins = dve.bn_stats(stats[:, t, :], src[:, t, :])
                    return ins

                def variances():
                    dve.memset(var_tmp[:, 0:1], 0.0)
                    for t in range(TB):
                        ins = dve.bn_aggr(aggr[:, t, :], stats[:, t, :])
                    step(ins)
                    step(dve.tensor_scalar(var[:, :], aggr[:, :, 1], LN_EPS, None, ALU.add))
                    seed_rsqrt(dve, chain, rstd[:, :], var[:, :])

                def nearer():
                    step(newton_rsqrt(dve, chain, rstd[:, :], var[:, :], var_tmp[:, :]))

                def normalise(dst, src, ts):
                    for t in ts:
                        ins = dve.tensor_scalar(dst[:, t, :], src[:, t, :], aggr[:, t, 0:1], rstd[:, t:t + 1],
                                                ALU.subtract, ALU.mult)
                    return ins

                def low(what, done, k_turn):
                    for c in range(CK):
                        slot, _, read, k = ring_slot((what, c))
                        dve.wait_ge(done.sem, done.at(k_turn, c + 1))
                        dve.tensor_tensor(h_lo[:, c, :], slot[:, :], h_hi[:, c, :].bitcast(F32), ALU.subtract)\
                           .then_inc(read.sem, 1)

                def rest(j):
                    dve.wait_ge(part0_done.sem, part0_done.at(ahead, j + 1))
                    dve.tensor_tensor(qk[:, j, :], qk[:, j, :], qk_part[:, j % 2, 0, :], ALU.subtract)\
                       .then_inc(rest_done.sem, 1)

                def part2(j):
                    dve.wait_ge(part1_done.sem, part1_done.at(ahead, j + 1))
                    dve.tensor_tensor(qk_part[:, j % 2, 2, :], qk[:, j, :], qk_part[:, j % 2, 1, :], ALU.subtract)\
                       .then_inc(qk_split.sem, 1)

                def take_values(p):
                    slot, full, read, k = ring_slot(("v", p))
                    dve.wait_ge(full.sem, full.at(ahead, k + 1))
                    for t in range(4):
                        ins = dve.tensor_tensor(v_t[:, 4 * p + t, :, 0:D1],
                                                slot[:, t * C:(t + 1) * C].rearrange("p (h d) -> p h d", d=D1),
                                                b_v[:, :].rearrange("p (h d) -> p h d", d=D1), ALU.add)
                    ins.then_inc(read.sem, 1)

                def reduce_units(g, units):
                    for u in units:
                        h, t, piece = UNITS[u]
                        slot, full, read, k = unit_slot(g, u)
                        cols = min(512, (t + 1) * P - 512 * piece)
                        col = unit_col(t, piece)
                        dve.wait_ge(full.sem, full.at(ahead if g == 0 else i, k + 1))
                        dve.reduce_max(mx[:, h, col:col + 1], slot[:, 0:cols], AX.X).then_inc(read.sem, 1)

                def maxima(g):
                    k = ahead if g == 0 else i
                    read, n_read = (unit0_read, NUNIT // 2) if g == 0 else (unit_read, g * NUNIT // 2)
                    for n in range(2):
                        dve.wait_ge(read[n].sem, read[n].at(k, n_read))
                    step(dve.tensor_scalar(mx_neg[:, :, :], mx[:, :, :], -1.0, None, ALU.mult))
                    step(dve.tensor_copy(nm[:, :, 0:PAIRED], mx_neg[:, :, 0:PAIRED]))
                    dve.tensor_tensor(nm[:, :, PAIRED:TB], mx_neg[:, :, PAIRED:UNIT_COLS:2],
                                      mx_neg[:, :, PAIRED + 1:UNIT_COLS:2], ALU.min).then_inc(nm_done[g].sem, 1)
                    dve.wait_ge(max_turned[g].sem, max_turned[g].at(k, 1))
                    if not lead:
                        stored = max_stored[(g - 1) % G1]
                        dve.wait_ge(stored.sem, stored.at(i, 1))
                    turned = misc[0:4 * TB, 0:P]
                    step(dve.tensor_copy(m_part[:, 0, :], turned))
                    dve.tensor_tensor(m_rest[:, :], turned, m_part[:, 0, :], ALU.subtract)\
                       .then_inc(max_taken[g].sem, 1)
                    dve.wait_ge(max_taken[g].sem, max_taken[g].at(k, 1))
                    step(dve.tensor_copy(m_part[:, 1, :], m_rest[:, :]))
                    step(dve.tensor_tensor(m_rest[:, :], m_rest[:, :], m_part[:, 1, :], ALU.subtract))
                    dve.tensor_copy(m_part[:, 2, :], m_rest[:, :]).then_inc(max_split[g].sem, 1)

                def copy_output(g, half):
                    dve.wait_ge(values_met.sem, values_met.at(i, g * NSTEP + (NSTEP if half else 4)))
                    dve.wait_ge(out_turned.sem, out_turned.at(i, 2 * g + half))
                    dve.tensor_copy(o_un[:, :], outp[:, :]).then_inc(out_read.sem, 1)

                def divide_output(g, half):
                    dve.wait_ge(out_turned.sem, out_turned.at(i, 2 * g + half + 1))
                    o = misc[:, :].rearrange("p (t h d) -> p t h d", t=4, h=4)
                    step(dve.reciprocal(o_rec[:, :, :], o[:, :, :, D1]))
                    dst = y[:, 4 * half:4 * half + 4, 4 * g * D1:(4 * g + 4) * D1]\
                        .rearrange("p t (h d) -> p t h d", h=4)
                    dve.tensor_tensor(dst, o[:, :, :, 0:D1], o_rec[:, :, :].unsqueeze(3).broadcast_to([P, 4, 4, D1]),
                                      ALU.mult).then_inc(out_taken.sem, 1)

                if lead:
                    dve.wait_ge(x_loaded.sem, x_loaded.at(ahead, 1))
                    step(statistics(xl, range(TB)))
                    variances()
                    for _ in range(3):
                        nearer()
                    normalise(xl, xl, range(TB)).then_inc(x_normed.sem, 1)
                    low("xT", xT_hi, ahead)
                    for j in range(2 * CK):
                        rest(j)
                        part2(j)
                    for p in range(2):
                        take_values(p)
                    reduce_units(0, range(NUNIT))
                    maxima(0)
                    chain.end()
                    return
                for g in range(G1):
                    nxt = (g + 1) % G1
                    if g == LAST - 1:
                        low("xT", xT_hi, ahead)
                    for n in range(NSTEP):
                        if g == LAST - 1 and n < 4 * CK and n % 2 == 1:
                            rest(n // 2)
                        if g == LAST - 1 and 0 < n <= 4 * CK and n % 2 == 0:
                            part2(n // 2 - 1)
                        reduce_units(nxt, units_in(nxt, n))
                        if g == 0 and n >= 8:
                            if n == 8:
                                dve.wait_ge(x_loaded.sem, x_loaded.at(ahead, 1))
                            ins = statistics(xl, range(2 * (n - 8), 2 * (n - 8) + 2))
                            if n == 11:
                                step(ins)
                        if g == 1 and n == 0:
                            variances()
                        if g == 1 and 1 <= n < 4:
                            nearer()
                        if g == 1 and 4 <= n < 8:
                            ins = normalise(xl, xl, range(2 * (n - 4), 2 * (n - 4) + 2))
                            if n == 7:
                                ins.then_inc(x_normed.sem, 1)
                        if n == AT_COPY1 and g > 0:
                            copy_output(g - 1, 1)
                        if n == AT_TURN1 and g > 0:
                            divide_output(g - 1, 1)
                        if n == AT_COPY0:
                            copy_output(g, 0)
                        if n == AT_TURN0:
                            if g == 0:
                                dve.wait_ge(f_stored.sem, f_stored.at(i, 0))
                            divide_output(g, 0)
                        if n == PASS1_AT[nxt][2]:
                            maxima(nxt)
                copy_output(LAST, 1)
                take_values(0)
                divide_output(LAST, 1)
                take_values(1)
                low("yT", yT_hi, i)
                for p in range(2):
                    slot, full, read, k = ring_slot(("wp", p))
                    dve.wait_ge(full.sem, full.at(i, k + 1))
                    dve.tensor_tensor(xl[:, 4 * p:4 * p + 4, :], slot[:, :].rearrange("p (t c) -> p t c", c=C),
                                      modb[:, 0:1, :].broadcast_to([P, 4, C]), ALU.mult).then_inc(read.sem, 1)
                dve.wait_ge(x1_done.sem, x1_done.at(i, 2))
                step(statistics(x1, range(TB)))
                variances()
                for _ in range(3):
                    nearer()
                normalise(y, x1, range(TB)).then_inc(x1_normed.sem, 1)
                chain.end()

            program(None, 0, lead_steps, lead=True)

            def body(i):
                program(i, i + 1, dve_steps)

            loop(dve, body)


H2, D2, WIN = 8, 64, 128
NWIN = T // WIN
PAIRS = H2 // 2
NPP = NWIN * PAIRS
INNER = H2 * D2
HID = C * 4 * 2 // 3
HK = -(-HID // P)
HPAD = HK * P
HLAST = HID - (HK - 1) * P
QK_SCALE = 8.0
NORM_MIN = 1e-12
UNIT = 2
UT = UNIT * WIN
NU = NWIN // UNIT
FIRST = -6
TURN_LAG = 3
MEET_LAG = TURN_LAG + 1
OUT_LAG = MEET_LAG + 1
E_RING = TURN_LAG + 1
STEPS = NPP + OUT_LAG
F_LATER = FIRST + 3


def rotary_tables():
    f = np.float32
    half = np.arange(0, D2, 2, dtype=f)
    freqs = np.arange(T, dtype=f)[:, None] * (f(1.0) / f(10000.0) ** (half / f(D2)))[None, :]
    base = (half + f(0.4 * D2)) / f(1.4 * D2)
    scale = base[None, :] ** ((np.arange(T, dtype=f) - f(T // 2)) / f(WIN // 2))[:, None]
    two = lambda a, b: np.concatenate([a, b], axis=1).astype(f)
    cos, sin, scale = two(np.cos(freqs), np.cos(freqs)), two(-np.sin(freqs), np.sin(freqs)), two(scale, scale)
    return np.stack([cos * scale, sin * scale, cos / scale, sin / scale]).astype(f)


def plan_mlp():
    plan = {}
    put = lambda step, *piece: plan.setdefault(step, []).append(piece)
    for u, s in ((-1, FIRST), (0, 13), (1, 21), (2, 28)):
        per_step = 2
        s += 1
        put(s - 1, "moments", u, None)
        put(s, "norm", u, None)
        put(s + 1, "hT", u, None)
        for m in range(HK):
            put(s + 2 + m // per_step, "ag", u, m)
        end = s + 2 + HK // per_step + int(u < 0)
        put(end, "gelu", u, None)
        put(end + 1, "product", u, None)
        put(min(end + 3, STEPS - 1), "w2", u, None)
    assert max(plan) < STEPS and sum(len(x) for x in plan.values()) == NU * (6 + HK)
    return plan


MLP_AT = plan_mlp()


def plan_fills():
    slots = {name: [] for name in ("p", "t", "s0", "s1", "et", "ot", "m0", "m1")}
    n_m = 0
    for pp in range(FIRST, STEPS):
        if pp in (FIRST, F_LATER):
            slots["et"].append(("fT", int(pp == F_LATER), 0))
            slots["ot"].append(("fT", int(pp == F_LATER), 1))
        for what, step in (("q", -6), ("k", -5), ("v", 0)):
            if (pp - step) % PAIRS == 0 and 0 <= (pp - step) // PAIRS < NWIN:
                slots["p"].append((what, (pp - step) // PAIRS))
        if pp % PAIRS == PAIRS - 1 and 0 <= (pp + 1) // PAIRS < NWIN:
            slots["t"] += [("qT", (pp + 1) // PAIRS), ("kT", (pp + 1) // PAIRS)]
        if 0 <= pp < NPP:
            slots[f"s{pp % 2}"].append(("s", pp))
        for piece, u, m in sorted(MLP_AT.get(pp, ()), key=lambda x: x[0] == "hT"):
            if piece in ("ag", "w2", "hT"):
                slots[f"m{n_m % 2}"].append((piece, u, m))
                n_m += 1
        if 0 <= pp - TURN_LAG < NPP:
            slots["et"].append(("et", pp - TURN_LAG))
        if 0 <= pp - MEET_LAG < NPP and (pp - MEET_LAG) % PAIRS == 0:
            slots["ot"].append(("oT", (pp - MEET_LAG) // PAIRS))
        if 0 <= pp - OUT_LAG < NPP and (pp - OUT_LAG) % PAIRS == PAIRS - 1:
            slots["t"].append(("wo", (pp - OUT_LAG) // PAIRS))
    return slots


FILLS = plan_fills()
FILL_AT = {f: (name, n, sum(1 for x in fills[:n] if x[0] != "oT"))
           for name, fills in FILLS.items() for n, f in enumerate(fills)}


def layer_stage(nc, sems, pre, f_in, f_out, tables, wqkv, qs, ks, wo, lg, lb, w1, b1, w2, b2, mod_dram, x1_dram, turns,
                final):
    with ExitStack() as ctx:
        sb = lambda name, shape, dt=F32: ctx.enter_context(nc.sbuf_tensor(f"{pre}_{name}", shape, dt))
        ps = lambda name, shape, dt=F32: ctx.enter_context(nc.psum_tensor(f"{pre}_{name}", shape, dt))
        sig = lambda name, per, by=1: Signal(sems, nc, f"{pre}_{name}", per, by)
        plain = lambda name: sems.enter_context(nc.semaphore(f"{pre}_{name}"))

        part = lambda name, shape: [sb(f"{name}_{x}", shape, F32R) for x in ("hi", "lo")]
        wqkv_p = part("wqkv", [P, CK, 3 * INNER])
        wo_p = part("wo", [P, PAIRS, C])
        w1_p = part("w1", [P, CK, 2, HPAD])
        w2_p = part("w2", [P, HK, C])
        tab = sb("tab", [P, 2, 2, NWIN, D2])
        qk_scale = sb("qk_scale", [P, 2, D2])
        ln_g = sb("ln_g", [P, CK])
        ln_b = sb("ln_b", [P, CK])
        b1_c = sb("b1_c", [P, 2, HK])
        b2_r = sb("b2_r", [P, 1, C])
        gate_r = sb("gate_r", [P, 1, C]) if final else None
        ident = sb("ident", [P, P])
        ident_bf = sb("ident_bf", [P, P], BF16)
        mask = sb("mask", [P, 2, 2 * WIN], BF16)

        fl = sb("fl", [P, TB, C])
        fr = sb("fr", [P, TB, C])
        x1_l = sb("x1_l", [P, UNIT, C]) if final else None
        hs = sb("hs", [P, TB, P])
        turned = part("turned", [P, CK, T + 2])
        qk = sb("qk", [P, 2, H2, D2])
        sq = sb("sq", [P, 2 * H2, D2])
        rot = sb("rot", [P, 2, H2, D2])
        qk_rot = sb("qk_rot", [P, 2, H2, D2])
        sums = sb("sums", [P, NWIN, 2 * H2])
        inv = sb("inv", [P, NWIN, 2 * H2])
        inv_tmp = sb("inv_tmp", [P, 2 * H2])
        scale_q = sb("scale_q", [P, NWIN, H2])
        v = sb("v", [P, 3, H2, D2])
        q_t = sb("q_t", [P, 2, PAIRS, WIN])
        k_t = sb("k_t", [P, 3, H2, WIN])
        top = sb("top", [P, NPP, 2])
        bias = sb("bias", [P, NPP, 2])
        total = sb("total", [P, NPP, 2])
        share = sb("share", [P, NPP, 2])
        e = sb("e", [P, E_RING, 2, 2 * WIN])
        e_t = sb("e_t", [P, 2, 4, WIN])
        o_p = part("o", [P, PAIRS, WIN])
        stats = sb("stats", [P, UNIT, 2, 6])
        aggr = sb("aggr", [P, UNIT, 2])
        var = sb("var", [P, UNIT])
        var_tmp = sb("var_tmp", [P, UNIT])
        rstd = sb("rstd", [P, UNIT])
        hn = sb("hn", [P, UNIT, C])
        h_scaled = sb("h_scaled", [P, CK, UT])
        h_t = part("h_t", [P, CK, UT])
        ag = sb("ag", [P, HK, 2, UT])
        hid_p = part("hid", [P, HK, UT])
        flat = lambda x, names: x.rearrange(f"p {names} -> p ({names})")
        fr_flat, ag_flat = flat(fr[:, :, :], "t c"), flat(ag[:, :, :, :], "m a t")

        bank = {name: ps("bank_" + name, [P, 512]) for name in FILLS}
        full = {n: sig(f"full_{n}", sum(1 for f in fills if f[0] != "oT")) for n, fills in FILLS.items()}
        read = {n: sig(f"read_{n}", len(fills)) for n, fills in FILLS.items()}

        const_made = plain("const_made")
        stage_zero = plain("stage_zero")
        raw_loaded = [plain(f"raw_loaded{n}") for n in range(7)]
        hi_split = plain("hi_split")
        lo_split = plain("lo_split")
        small_loaded = plain("small_loaded")
        tab_made = plain("tab_made")
        f_loaded = [sig(f"f_loaded{half}", 2, 16) for half in range(2)]
        gate_loaded = sig("gate_loaded", 1, 16)
        x1_loaded = sig("x1_loaded", NU, 16)
        f_hi = sig("f_hi", 4)
        squared = sig("squared", NWIN)
        summed = sig("summed", NWIN)
        inv_done = sig("inv_done", NWIN)
        turned_parts = sig("turned_parts", NWIN)
        summed_parts = sig("summed_parts", 2 * NWIN)
        rotated = sig("rotated", NWIN)
        bias_done = sig("bias_done", NPP)
        share_done = sig("share_done", NPP)
        e_done = sig("e_done", NPP)
        pairs_met = sig("pairs_met", NPP)
        o_hi = sig("o_hi", NWIN)
        shifted = sig("shifted", 2 * NWIN - 1, 16)
        normed = sig("normed", NU)
        h_ready = sig("h_ready", 2 * NU)
        h_hi = sig("h_hi", NU)
        h_lo = sig("h_lo", NU)
        gelu_done = sig("gelu_done", HK * NU)
        multiplied = sig("multiplied", 2 * NU)
        hid_hi = sig("hid_hi", 2 * NU)
        hid_lo = sig("hid_lo", 2 * NU)
        b2_added = sig("b2_added", NU)
        gated = sig("gated", NU)
        finished = sig("finished", NU)
        f_stored = [sig(f"f_stored{u}", 1, 16) for u in range(NU)]
        dve_steps = Chain(sems, nc, f"{pre}_dve_steps", 14 * NU + 12 * NWIN + NPP)
        prime(nc, sems.signals)
        block = ctx.enter_context(nc.Block())

        def loop(eng, body):
            if turns == 1:
                body(0)
            else:
                with eng.Fori(0, turns) as i:
                    body(i)
            body(turns, closing=True)

        def pieces_at(pp, closing):
            return [x for x in MLP_AT.get(pp, ()) if x[1] < 0 or not closing]

        sample_before = lambda i, closing: turns - 1 if closing or turns == 1 else (i + (turns - 1)) % turns
        blocks_of = lambda u: slice(UNIT * (u % NU), UNIT * (u % NU) + UNIT)

        rows_of = lambda dram, i, u: dram[i, UT * (u % NU):UT * (u % NU + 1), :].rearrange("(t p) c -> p t c", p=P)
        w1_raw = [x[:, 0:2 * HPAD].rearrange("p (a n) -> p a n", a=2) for x in (fr_flat, ag_flat)]
        wqkv_raw = [flat(e[:, :, :, :], "n h s")[:, 0:3 * INNER], flat(v[:, :, :, :], "w h d")]
        wo_raw = flat(qk[:, :, :, :], "a h d").rearrange("p (k c) -> p k c", c=C)
        w2_raw = ag_flat[:, 2 * HPAD:2 * HPAD + (HK - 1) * C].rearrange("p (k c) -> p k c", c=C)
        w2_tail = flat(hs[:, 0:2, :], "t c")
        pieces = [(wqkv_raw[n], wqkv_p[0][:, n, :], wqkv_p[1][:, n, :]) for n in range(CK)]
        pieces += [(w1_raw[n], w1_p[0][:, n, :, :], w1_p[1][:, n, :, :]) for n in range(CK)]
        pieces += [(w2_tail, w2_p[0][:, HK - 1, :], w2_p[1][:, HK - 1, :]),
                   (wo_raw, wo_p[0][:, :, :], wo_p[1][:, :, :]),
                   (w2_raw, w2_p[0][:, 0:HK - 1, :], w2_p[1][:, 0:HK - 1, :])]
        W1_PIECE, TAIL_PIECE = CK, 2 * CK
        n_loads = [2 if W1_PIECE <= n < TAIL_PIECE else 1 for n in range(len(pieces))]
        NSMALL = 4 + 2 + 2 + 4 + 1
        n_const = 11 + int(final)

        @block.sync
        def _(sp):
            for n in range(CK):
                sp.dma_start(wqkv_raw[n], wqkv[n * P:(n + 1) * P, :]).then_inc(raw_loaded[n], 16)
            for u in range(NU):
                sp.dma_start(fl[:, blocks_of(u), :], rows_of(f_in, 0, u)).then_inc(f_loaded[u // 2].sem, 16)
            sp.wait_ge(stage_zero, 5)
            for n in range(CK):
                for a in range(2):
                    sp.dma_start(w1_raw[n][:, a, 0:HID], w1[n * P:(n + 1) * P, a * HID:(a + 1) * HID])\
                      .then_inc(raw_loaded[W1_PIECE + n], 16)
            sp.dma_start(w2_tail[0:HLAST, :], w2[(HK - 1) * P:HID, :]).then_inc(raw_loaded[TAIL_PIECE], 16)
            sp.dma_start(wo_raw, wo.rearrange("(k p) c -> p k c", p=P)).then_inc(raw_loaded[TAIL_PIECE + 1], 16)
            sp.dma_start(w2_raw, w2[0:(HK - 1) * P, :].rearrange("(k p) c -> p k c", p=P))\
              .then_inc(raw_loaded[TAIL_PIECE + 2], 16)
            for n in range(4):
                sp.dma_start(tab[:, n // 2, n % 2, :, :], tables[n].rearrange("(w p) d -> p w d", p=P))\
                  .then_inc(small_loaded, 16)
            sp.dma_start(qk_scale[:, 0, :], qs.partition_broadcast(P)).then_inc(small_loaded, 16)
            sp.dma_start(qk_scale[:, 1, :], ks.partition_broadcast(P)).then_inc(small_loaded, 16)
            with nc.allow_non_contiguous_dma(reason="vectors that go one value to a partition"):
                sp.dma_start(ln_g[:, :], lg.rearrange("(k p) -> p k", p=P)).then_inc(small_loaded, 16)
                sp.dma_start(ln_b[:, :], lb.rearrange("(k p) -> p k", p=P)).then_inc(small_loaded, 16)
                for a in range(2):
                    sp.dma_start(b1_c[:, a, 0:HK - 1], b1[a * HID:a * HID + (HK - 1) * P]
                                 .rearrange("(m p) -> p m", p=P)).then_inc(small_loaded, 16)
                    sp.dma_start(b1_c[0:HLAST, a, HK - 1:HK], b1[a * HID + (HK - 1) * P:(a + 1) * HID]
                                 .rearrange("(p m) -> p m", m=1)).then_inc(small_loaded, 16)
            sp.dma_start(b2_r[:, 0, :], b2.partition_broadcast(P)).then_inc(small_loaded, 16)

            def body(i, closing=False):
                before = sample_before(i, closing)
                if final:
                    sp.wait_ge(finished.sem, finished.before(i, NU))
                    sp.dma_start(x1_l[:, :, :], rows_of(x1_dram, before, -1)).then_inc(x1_loaded.sem, 16)
                for pp in range(FIRST, STEPS):
                    if not closing and 0 <= pp - OUT_LAG < NPP and (pp - OUT_LAG) % PAIRS == PAIRS - 1:
                        w = (pp - OUT_LAG) // PAIRS
                        _, n, _ = FILL_AT[("wo", w)]
                        sp.wait_ge(read["t"].sem, read["t"].at(i, n + 1))
                        sp.dma_start(hs[1:P, w, :], fr[0:P - 1, w, P:C]).then_inc(shifted.sem, 16)
                        if w + 1 < NWIN:
                            sp.dma_start(hs[0:1, w + 1, :], fr[P - 1:P, w, P:C]).then_inc(shifted.sem, 16)
                        if w % UNIT == UNIT - 1:
                            u = w // UNIT
                            nxt = 0 if turns == 1 else (i + 1) % turns
                            sp.dma_start(fl[:, blocks_of(u), :], rows_of(f_in, nxt, u))\
                              .then_inc(f_loaded[u // 2].sem, 16)
                    for piece, u, m in pieces_at(pp, closing):
                        if piece != "w2":
                            continue
                        name, n, _ = FILL_AT[(piece, u, m)]
                        if final:
                            sp.wait_ge(finished.sem, finished.at(i, u + 2))
                        else:
                            sp.wait_ge(read[name].sem, read[name].at(i, n + 1))
                        sp.dma_start(rows_of(f_out, before if u < 0 else i, u), fr[:, blocks_of(u), :])\
                          .then_inc(f_stored[u % NU].sem, 16)
                        if final and not closing:
                            if u == -1:
                                sp.dma_start(gate_r[:, 0, :], mod_dram[i, NMOD - 1, :].partition_broadcast(P))\
                                  .then_inc(gate_loaded.sem, 16)
                            if u + 1 < NU - 1:
                                sp.dma_start(x1_l[:, :, :], rows_of(x1_dram, i, u + 1)).then_inc(x1_loaded.sem, 16)

            loop(sp, body)
            for u in range(NU):
                sp.wait_ge(f_stored[u].sem, f_stored[u].at(turns, int(u == NU - 1)))
            for half in range(2):
                sp.wait_ge(f_loaded[half].sem, f_loaded[half].at(turns, 2))

        @block.gpsimd
        def _(pool):
            for raw in w1_raw:
                pool.memset(raw[:, :, HID:HPAD], 0.0).then_inc(stage_zero, 1)
            pool.memset(fr[:, TB - UNIT:TB, :], 0.0).then_inc(stage_zero, 1)
            pool.memset(hs[:, :, :], 0.0).then_inc(stage_zero, 1)
            pool.memset(b1_c[:, :, :], 0.0).then_inc(stage_zero, 1)
            pool.memset(ident[:, :], 0.0).then_inc(const_made, 1)
            pool.memset(ident_bf[:, :], 0.0).then_inc(const_made, 1)
            pool.memset(mask[:, :, :], 0.0).then_inc(const_made, 1)
            pool.memset(k_t[:, :, :, :], 0.0).then_inc(const_made, 1)
            for t in turned:
                pool.memset(t[:, :, 0:1].bitcast(F32), 0.0).then_inc(const_made, 1)
            if final:
                pool.memset(gate_r[:, :, :], 0.0).then_inc(const_made, 1)
            pool.wait_ge(const_made, 6 + int(final))
            for m in (ident, ident_bf):
                pool.affine_select(out=m[:, :], in_=m[:, :], compare_op=ALU.not_equal, fill=1.0, base=0,
                                   pattern=[[-1, P]], channel_multiplier=1).then_inc(const_made, 1)
            pool.affine_select(out=mask[:, :, 0:WIN], in_=mask[:, :, 0:WIN], compare_op=ALU.is_ge, fill=MASKED,
                               base=0, pattern=[[0, 2], [1, WIN]], channel_multiplier=-1).then_inc(const_made, 1)
            pool.affine_select(out=mask[:, :, WIN:2 * WIN], in_=mask[:, :, WIN:2 * WIN], compare_op=ALU.is_ge,
                               fill=MASKED, base=0, pattern=[[0, 2], [-1, WIN]], channel_multiplier=1)\
                .then_inc(const_made, 1)
            pool.wait_ge(small_loaded, 16 * NSMALL)
            for a in range(2):
                scales = qk_scale[:, a, :].rearrange("p (r d) -> p r d", r=2)
                for r, view in ((0, scales), (1, scales[:, ::-1, :])):
                    t = tab[:, a, r, :, :].rearrange("p w (r d) -> p w r d", r=2)
                    pool.tensor_tensor(t, t, view.unsqueeze(1).broadcast_to([P, NWIN, 2, D2 // 2]), ALU.mult)\
                        .then_inc(tab_made, 1)
            pool.wait_ge(lo_split, TAIL_PIECE + 1)
            pool.memset(hs[0:1, 0, :], 0.0).then_inc(const_made, 1)
            pool.wait_ge(const_made, n_const)

            def body(i, closing=False):

                def rotate(w):
                    pool.wait_ge(turned_parts.sem, turned_parts.at(i, w + 1))
                    for a in range(2):
                        pool.tensor_tensor(qk_rot[:, a, :, :], qk_rot[:, a, :, :], rot[:, a, :, :], ALU.add)\
                            .then_inc(summed_parts.sem, 1)

                def scale_k(w):
                    pool.wait_ge(summed_parts.sem, summed_parts.at(i, 2 * w + 2))
                    pool.wait_ge(inv_done.sem, inv_done.at(i, w + 1))
                    pool.tensor_tensor(qk_rot[:, 1, :, :], qk_rot[:, 1, :, :],
                                       inv[:, w, H2:2 * H2].unsqueeze(2).broadcast_to([P, H2, D2]), ALU.mult)\
                        .then_inc(rotated.sem, 1)

                def share_out(pp):
                    lo = WIN if pp < PAIRS else 0
                    pool.wait_ge(share_done.sem, share_done.at(i, pp + 1))
                    weights = e[:, pp % E_RING, :, lo:]
                    pool.tensor_tensor(weights, weights, share[:, pp, :].unsqueeze(2)
                                       .broadcast_to([P, 2, 2 * WIN - lo]), ALU.mult).then_inc(e_done.sem, 1)

                def piece_of_mlp(piece, u, m):
                    if piece == "hT":
                        pool.wait_ge(h_hi.sem, h_hi.at(i, u + 2))
                        pool.tensor_tensor(h_t[1][:, :, :], h_scaled[:, :, :], h_t[0][:, :, :].bitcast(F32),
                                           ALU.subtract).then_inc(h_lo.sem, 1)
                        pool.wait_ge(normed.sem, normed.at(i, u + 2))
                        rows = fr[:, blocks_of(u), :]
                        pool.tensor_tensor(rows, rows, b2_r[:, :, :].broadcast_to([P, UNIT, C]), ALU.add)\
                            .then_inc(b2_added.sem, 1)
                    elif piece == "product":
                        for half in range(2):
                            ms = slice(HK // 2 * half, HK // 2 * (half + 1))
                            pool.wait_ge(hid_hi.sem, hid_hi.at(i, 2 * (u + 1) + half + 1))
                            pool.tensor_tensor(hid_p[1][:, ms, :], ag[:, ms, 0, :], hid_p[0][:, ms, :].bitcast(F32),
                                               ALU.subtract).then_inc(hid_lo.sem, 1)
                    elif piece == "w2" and final:
                        name, n, _ = FILL_AT[(piece, u, m)]
                        pool.wait_ge(read[name].sem, read[name].at(i, n + 1))
                        if u >= 0:
                            pool.wait_ge(gate_loaded.sem, gate_loaded.at(i, 1))
                        pool.wait_ge(x1_loaded.sem, x1_loaded.at(i, u + 2))
                        rows = fr[:, blocks_of(u), :]
                        pool.tensor_tensor(rows, rows, gate_r[:, :, :].broadcast_to([P, UNIT, C]), ALU.mult)\
                            .then_inc(gated.sem, 1)
                        pool.wait_ge(gated.sem, gated.at(i, u + 2))
                        pool.tensor_tensor(rows, rows, x1_l[:, :, :], ALU.add).then_inc(finished.sem, 1)

                for pp in range(FIRST, STEPS):
                    if not closing:
                        if 0 <= pp - 1 < NPP:
                            share_out(pp - 1)
                        if pp % PAIRS == 1 and (pp + 3) // PAIRS < NWIN:
                            rotate((pp + 3) // PAIRS)
                        if pp % PAIRS == 2 and 0 <= (pp + 2) // PAIRS < NWIN:
                            scale_k((pp + 2) // PAIRS)
                    for x in pieces_at(pp, closing):
                        piece_of_mlp(*x)

            loop(pool, body)

        @block.scalar
        def _(act):
            for n, (raw, hi, lo) in enumerate(pieces):
                act.wait_ge(raw_loaded[n], 16 * n_loads[n])
                act.activation(hi, raw, ACT.Copy).then_inc(hi_split, 1)
            act.wait_ge(const_made, n_const - 1)
            act.wait_ge(lo_split, len(pieces))
            act.wait_ge(small_loaded, 16 * NSMALL)

            def body(i, closing=False):
                def wait_full(what):
                    name, n, k = FILL_AT[what]
                    act.wait_ge(full[name].sem, full[name].at(i, k + 1))
                    return bank[name], read[name].sem

                def take_projected(what, w):
                    src, back = wait_full((what, w))
                    if what == "v":
                        if w >= 3:
                            act.wait_ge(pairs_met.sem, pairs_met.at(i, PAIRS * (w - 1)))
                        act.activation(v[:, w % 3, :, :].rearrange("p h d -> p (h d)"), src[:, :], ACT.Copy)\
                            .then_inc(back, 1)
                        return
                    if w and what == "q":
                        act.wait_ge(turned_parts.sem, turned_parts.at(i, w))
                    act.activation(qk[:, int(what == "k"), :, :].rearrange("p h d -> p (h d)"), src[:, :], ACT.Copy)\
                        .then_inc(back, 1)

                def take_q(w):
                    src, back = wait_full(("qT", w))
                    act.activation(q_t[:, w % 2, :, :].rearrange("p a t -> p (a t)"), src[:, :], ACT.Copy).then_inc(back, 1)

                def take_k(w):
                    src, back = wait_full(("kT", w))
                    for hh in range(2):
                        rows = slice(D2 * hh, D2 * (hh + 1))
                        ins = act.activation(k_t[rows, w % 3, hh:H2:2, :],
                                             src[rows, :].rearrange("p (a t) -> p a t", a=PAIRS), ACT.Copy)
                    ins.then_inc(back, 1)

                def square(w):
                    _, n, _ = FILL_AT[("k", w)]
                    act.wait_ge(read["p"].sem, read["p"].at(i, n + 1))
                    if w:
                        act.wait_ge(summed.sem, summed.at(i, w))
                    act.activation(sq[:, :, :].rearrange("p h d -> p (h d)"),
                                   qk[:, :, :, :].rearrange("p a h d -> p (a h d)"), ACT.Square)\
                        .then_inc(squared.sem, 1)

                def exponentials(pp):
                    w = pp // PAIRS
                    src, back = wait_full(("s", pp))
                    act.wait_ge(bias_done.sem, bias_done.at(i, pp + 1))
                    if pp >= E_RING:
                        _, _, k = FILL_AT[("et", pp - E_RING)]
                        act.wait_ge(full["et"].sem, full["et"].at(i, k + 1))
                    lo = WIN if w == 0 else 0
                    for hh in range(2):
                        h = 2 * (pp % PAIRS) + hh
                        ins = act.activation(e[:, pp % E_RING, hh, lo:], src[:, 2 * WIN * hh + lo:2 * WIN * (hh + 1)],
                                             ACT.Exp, scale=scale_q[:, w, h:h + 1], bias=bias[:, pp, hh:hh + 1],
                                             accum_out=total[:, pp, hh:hh + 1])
                    ins.then_inc(back, 1)

                def values_hi(w):
                    act.wait_ge(pairs_met.sem, pairs_met.at(i, PAIRS * (w + 1)))
                    if w:
                        _, _, k = FILL_AT[("wo", w - 1)]
                        act.wait_ge(full["t"].sem, full["t"].at(i, k + 1))
                    act.activation(o_p[0][:, :, :].rearrange("p a t -> p (a t)"), bank["ot"][:, :], ACT.Copy)\
                        .then_inc(o_hi.sem, 1)

                def piece_of_mlp(piece, u, m):
                    if piece == "hT":
                        act.wait_ge(h_ready.sem, h_ready.at(i, 2 * (u + 2)))
                        act.activation(h_t[0][:, :, :], h_scaled[:, :, :], ACT.Copy).then_inc(h_hi.sem, 1)
                    elif piece == "ag":
                        if m == 0:
                            act.wait_ge(hid_lo.sem, hid_lo.at(i, 2 * (u + 1)))
                        src, back = wait_full((piece, u, m))
                        act.activation(ag[:, m, :, :].rearrange("p a t -> p (a t)"), src[:, :], ACT.Copy)\
                            .then_inc(back, 1)
                    elif piece == "gelu":
                        for m in range(HK):
                            name, n, _ = FILL_AT[("ag", u, m)]
                            act.wait_ge(read[name].sem, read[name].at(i, n + 1))
                            act.activation(ag[:, m, 1, :], ag[:, m, 1, :], ACT.Gelu, bias=b1_c[:, 1, m:m + 1])\
                                .then_inc(gelu_done.sem, 1)
                    elif piece == "product":
                        for half in range(2):
                            ms = slice(HK // 2 * half, HK // 2 * (half + 1))
                            act.wait_ge(multiplied.sem, multiplied.at(i, 2 * (u + 1) + half + 1))
                            act.activation(hid_p[0][:, ms, :], ag[:, ms, 0, :], ACT.Copy).then_inc(hid_hi.sem, 1)

                for pp in range(FIRST, STEPS):
                    if not closing:
                        if pp in (FIRST, F_LATER):
                            half = int(pp == F_LATER)
                            for c in range(CK):
                                src, _ = wait_full(("fT", half, c))
                                act.activation(turned[0][:, c, 1 + 512 * half:513 + 512 * half], src[:, :], ACT.Copy)\
                                    .then_inc(f_hi.sem, 1)
                        if pp % PAIRS == 2 and (pp + 6) // PAIRS < NWIN:
                            take_projected("q", (pp + 6) // PAIRS)
                        if pp % PAIRS == 3 and (pp + 5) // PAIRS < NWIN:
                            take_projected("k", (pp + 5) // PAIRS)
                        if pp % PAIRS == 0 and 0 <= pp < NPP:
                            take_projected("v", pp // PAIRS)
                        if pp % PAIRS == 3 and 0 <= (pp + 1) // PAIRS < NWIN:
                            take_q((pp + 1) // PAIRS)
                        if 0 <= pp < NPP:
                            exponentials(pp)
                        if pp % PAIRS == 3 and 0 <= (pp + 1) // PAIRS < NWIN:
                            take_k((pp + 1) // PAIRS)
                        if pp % PAIRS == 3 and (pp + 5) // PAIRS < NWIN:
                            square((pp + 5) // PAIRS)
                        if 0 <= pp - TURN_LAG < NPP and pp % 4 != 3:
                            take_turned(act, i, pp - TURN_LAG)
                        if 0 <= pp - MEET_LAG < NPP and (pp - MEET_LAG) % PAIRS == PAIRS - 1:
                            values_hi((pp - MEET_LAG) // PAIRS)
                    for x in pieces_at(pp, closing):
                        piece_of_mlp(*x)

            def take_turned(eng, i, pp):
                name, n, k = FILL_AT[("et", pp)]
                eng.wait_ge(full[name].sem, full[name].at(i, k + 1))
                if pp >= 2:
                    eng.wait_ge(pairs_met.sem, pairs_met.at(i, pp - 1))
                lo = 1 if pp < PAIRS else 0
                dst = e_t[:, pp % 2, :, :].rearrange("p (h b) t -> p h b t", h=2)[:, :, lo:, :]
                src = bank[name][:, :].rearrange("p (h b t) -> p h b t", h=2, b=2)[:, :, lo:, :]
                eng.activation(dst, src, ACT.Copy).then_inc(read[name].sem, 1)

            loop(act, body)

        @block.tensor
        def _(pe):
            pe.wait_ge(const_made, n_const - 1)
            pe.wait_ge(lo_split, len(pieces))

            def body(i, closing=False):
                def fill(what):
                    name, n, _ = FILL_AT[what]
                    pe.wait_ge(read[name].sem, read[name].at(i, n))
                    return bank[name], full[name].sem

                def read_of(what):
                    name, n, _ = FILL_AT[what]
                    pe.wait_ge(read[name].sem, read[name].at(i, n + 1))

                def three(out, lhs, rhs, first, last):
                    for j, (a, b) in enumerate(((0, 0), (0, 1), (1, 0))):
                        mm = pe.matmul(out, lhs(a), rhs(b), start=(first and j == 0), stop=(last and j == 2))
                    return mm

                def turn_f(half):
                    pe.wait_ge(f_loaded[half].sem, f_loaded[half].at(i, 2))
                    for c in range(CK):
                        slot, done = fill(("fT", half, c))
                        for t in range(4):
                            mm = pe.transpose(slot[:, t * P:(t + 1) * P], fl[:, 4 * half + t, c * P:(c + 1) * P],
                                              ident[:, :])
                        mm.then_inc(done, 1)

                def project(what, w):
                    if what == "q" and w % 4 == 0:
                        read_of(("fT", w // 4, 0))
                        read_of(("fT", w // 4, 1))
                    slot, done = fill((what, w))
                    at = INNER * "qkv".index(what)
                    for c in range(CK):
                        tok = slice(w * WIN + 1 - c, (w + 1) * WIN + 1 - c)
                        mm = three(slot[:, :], lambda a: turned[a][:, c, tok], lambda b: wqkv_p[b][:, c, at:at + INNER],
                                   c == 0, c == CK - 1)
                    mm.then_inc(done, 1)

                def turn_qk(what, w):
                    a = int(what == "kT")
                    if a:
                        pe.wait_ge(rotated.sem, rotated.at(i, w + 1))
                    else:
                        pe.wait_ge(summed_parts.sem, summed_parts.at(i, 2 * w + 1))
                    slot, done = fill((what, w))
                    for p in range(PAIRS):
                        mm = pe.transpose(slot[:, p * P:(p + 1) * P],
                                          qk_rot[:, a, 2 * p:2 * p + 2, :].rearrange("p h d -> p (h d)"),
                                          ident[:, :])
                    mm.then_inc(done, 1)

                def scores(pp):
                    w, p = pp // PAIRS, pp % PAIRS
                    if p == 0:
                        read_of(("kT", w))
                    slot, done = fill(("s", pp))
                    for hh in range(2):
                        for b in range(1 if w == 0 else 0, 2):
                            at = (2 * hh + b) * WIN
                            mm = pe.matmul(slot[:, at:at + WIN], q_t[:, w % 2, p, :], k_t[:, (w - 1 + b) % 3, 2 * p + hh, :],
                                           start=True, stop=False)
                            mm = pe.matmul(slot[:, at:at + WIN], ident_bf[:, :], mask[:, hh, b * WIN:(b + 1) * WIN],
                                           start=False, stop=True)
                    mm.then_inc(done, 1)

                def turn_weights(pp):
                    pe.wait_ge(e_done.sem, e_done.at(i, pp + 1))
                    slot, done = fill(("et", pp))
                    for hh in range(2):
                        for b in range(1 if pp < PAIRS else 0, 2):
                            at = (2 * hh + b) * WIN
                            mm = pe.transpose(slot[:, at:at + WIN], e[:, pp % E_RING, hh, b * WIN:(b + 1) * WIN],
                                              ident[:, :])
                    mm.then_inc(done, 1)

                def meet_values(pp):
                    w, p = pp // PAIRS, pp % PAIRS
                    read_of(("et", pp))
                    if p == 0:
                        slot, _ = fill(("oT", w))
                        read_of(("v", w))
                    first = 1 if w == 0 else 0
                    for hh in range(2):
                        for b in range(first, 2):
                            mm = pe.matmul(bank["ot"][D2 * hh:D2 * (hh + 1), p * WIN:(p + 1) * WIN],
                                           v[:, (w - 1 + b) % 3, 2 * p + hh, :], e_t[:, pp % 2, 2 * hh + b, :],
                                           start=(b == first), stop=(b == 1))
                    mm.then_inc(pairs_met.sem, 1)

                def project_out(w):
                    read_of(("oT", w))
                    slot, done = fill(("wo", w))
                    for p in range(PAIRS):
                        mm = three(slot[:, 0:C], lambda a: o_p[a][:, p, :], lambda b: wo_p[b][:, p, :],
                                   p == 0, p == PAIRS - 1)
                    mm.then_inc(done, 1)

                def piece_of_mlp(piece, u, m):
                    if piece == "hT":
                        pe.wait_ge(normed.sem, normed.at(i, u + 2))
                        slot, done = fill((piece, u, m))
                        for c in range(CK):
                            for t in range(UNIT):
                                at = c * UT + t * P
                                mm = pe.transpose(slot[:, at:at + P], hn[:, t, c * P:(c + 1) * P], ident[:, :])
                        mm.then_inc(done, 1)
                    elif piece == "ag":
                        pe.wait_ge(h_lo.sem, h_lo.at(i, u + 2))
                        slot, done = fill((piece, u, m))
                        for a in range(2):
                            for c in range(CK):
                                mm = three(slot[:, a * UT:(a + 1) * UT], lambda b: w1_p[b][:, c, a, m * P:(m + 1) * P],
                                           lambda b: h_t[b][:, c, :], c == 0, c == CK - 1)
                        mm.then_inc(done, 1)
                    elif piece == "w2":
                        slot, done = fill((piece, u, m))
                        for t in range(UNIT):
                            for m in range(HK):
                                if t == 0 and m % (HK // 2) == 0:
                                    pe.wait_ge(hid_lo.sem, hid_lo.at(i, 2 * (u + 1) + m // (HK // 2) + 1))
                                mm = three(slot[:, t * C:(t + 1) * C], lambda a: hid_p[a][:, m, t * P:(t + 1) * P],
                                           lambda b: w2_p[b][:, m, :], m == 0, m == HK - 1)
                        mm.then_inc(done, 1)

                for pp in range(FIRST, STEPS):
                    if not closing:
                        if pp in (FIRST, F_LATER):
                            turn_f(int(pp == F_LATER))
                        if pp % PAIRS == 2 and (pp + 6) // PAIRS < NWIN:
                            project("q", (pp + 6) // PAIRS)
                        if pp % PAIRS == 3 and (pp + 5) // PAIRS < NWIN:
                            project("k", (pp + 5) // PAIRS)
                        if pp % PAIRS == 0 and 0 <= pp < NPP:
                            project("v", pp // PAIRS)
                        turns_qk = pp % PAIRS == 3 and 0 <= (pp + 1) // PAIRS < NWIN
                        if turns_qk:
                            turn_qk("qT", (pp + 1) // PAIRS)
                        if 0 <= pp < NPP:
                            scores(pp)
                        if turns_qk:
                            turn_qk("kT", (pp + 1) // PAIRS)
                        if 0 <= pp - TURN_LAG < NPP:
                            turn_weights(pp - TURN_LAG)
                        if 0 <= pp - MEET_LAG < NPP:
                            meet_values(pp - MEET_LAG)
                        if 0 <= pp - OUT_LAG < NPP and (pp - OUT_LAG) % PAIRS == PAIRS - 1:
                            project_out((pp - OUT_LAG) // PAIRS)
                    for x in sorted(pieces_at(pp, closing), key=lambda x: x[0] == "hT"):
                        piece_of_mlp(*x)

            loop(pe, body)

        @block.vector
        def _(dve):
            for n, (raw, hi, lo) in enumerate(pieces):
                dve.wait_ge(hi_split, n + 1)
                dve.tensor_tensor(lo, raw, hi.bitcast(F32), ALU.subtract).then_inc(lo_split, 1)
            dve.wait_ge(small_loaded, 16 * NSMALL)
            dve.wait_ge(tab_made, 4)
            dve.wait_ge(const_made, n_const)

            def body(i, closing=False):
                dve_steps.start(dve, i)
                step = dve_steps.step

                def wait_full(what):
                    name, n, k = FILL_AT[what]
                    dve.wait_ge(full[name].sem, full[name].at(i, k + 1))
                    return bank[name], read[name].sem

                def sum_squares(w):
                    dve.wait_ge(squared.sem, squared.at(i, w + 1))
                    step(dve.reduce_sum(sums[:, w, :], sq[:, :, :], AX.X))
                    dve.tensor_scalar(sums[:, w, :], sums[:, w, :], NORM_MIN ** 2, None, ALU.max)\
                       .then_inc(summed.sem, 1)

                def rotation_products(w):
                    _, n, _ = FILL_AT[("k", w)]
                    dve.wait_ge(read["p"].sem, read["p"].at(i, n + 1))
                    name, _, k = FILL_AT[("kT", w - 1)] if w else FILL_AT[("fT", 0, 1)]
                    dve.wait_ge(full[name].sem, full[name].at(i, k + 1))
                    cos = tab[:, :, 0, w, :].unsqueeze(2).broadcast_to([P, 2, H2, D2])
                    dve.tensor_tensor(qk_rot[:, :, :, :], qk[:, :, :, :], cos, ALU.mult)
                    for a in range(2):
                        x = qk[:, a, :, :].rearrange("p h (r d) -> p h r d", r=2)[:, :, ::-1, :]
                        sin = tab[:, a, 1, w, :].rearrange("p (r d) -> p r d", r=2).unsqueeze(1)\
                            .broadcast_to([P, H2, 2, D2 // 2])
                        ins = dve.tensor_tensor(rot[:, a, :, :].rearrange("p h (r d) -> p h r d", r=2), x, sin,
                                                ALU.mult)
                    ins.then_inc(turned_parts.sem, 1)

                def inverse_norms_begun(w):
                    dve.wait_ge(summed.sem, summed.at(i, w + 1))
                    seed_rsqrt(dve, dve_steps, inv[:, w, :], sums[:, w, :])
                    step(newton_rsqrt(dve, dve_steps, inv[:, w, :], sums[:, w, :], inv_tmp[:, :]))

                def inverse_norms(w):
                    step(newton_rsqrt(dve, dve_steps, inv[:, w, :], sums[:, w, :], inv_tmp[:, :]))
                    newton_rsqrt(dve, dve_steps, inv[:, w, :], sums[:, w, :], inv_tmp[:, :]).then_inc(inv_done.sem, 1)
                    dve.wait_ge(inv_done.sem, inv_done.at(i, w + 1))
                    step(dve.tensor_scalar(scale_q[:, w, :], inv[:, w, 0:H2], QK_SCALE, None, ALU.mult))

                def row_tops(pp):
                    w, p = pp // PAIRS, pp % PAIRS
                    src, _ = wait_full(("s", pp))
                    lo = WIN if w == 0 else 0
                    step(dve.reduce_max(top[:, pp, :], src[:, :].rearrange("p (h s) -> p h s", h=2)[:, :, lo:], AX.X))
                    dve.scalar_tensor_tensor(out=bias[:, pp, :], in0=top[:, pp, :], scalar=-1.0,
                                             in1=scale_q[:, w, 2 * p:2 * p + 2], op0=ALU.mult, op1=ALU.mult)\
                       .then_inc(bias_done.sem, 1)

                def shares(pp):
                    name, n, _ = FILL_AT[("s", pp)]
                    dve.wait_ge(read[name].sem, read[name].at(i, n + 1))
                    dve.reciprocal(share[:, pp, :], total[:, pp, :]).then_inc(share_done.sem, 1)

                def take_turned(pp):
                    src, back = wait_full(("et", pp))
                    if pp >= 2:
                        dve.wait_ge(pairs_met.sem, pairs_met.at(i, pp - 1))
                    lo = 1 if pp < PAIRS else 0
                    dve.tensor_copy(e_t[:, pp % 2, :, :].rearrange("p (h b) t -> p h b t", h=2)[:, :, lo:, :],
                                    src[:, :].rearrange("p (h b t) -> p h b t", h=2, b=2)[:, :, lo:, :])\
                        .then_inc(back, 1)

                def split_f(half):
                    for c in range(CK):
                        dve.wait_ge(f_hi.sem, f_hi.at(i, CK * half + c + 1))
                        name, _, _ = FILL_AT[("fT", half, c)]
                        cols = slice(1 + 512 * half, 513 + 512 * half)
                        dve.tensor_tensor(turned[1][:, c, cols], bank[name][:, :], turned[0][:, c, cols].bitcast(F32),
                                          ALU.subtract).then_inc(read[name].sem, 1)

                def values_lo(w):
                    dve.wait_ge(o_hi.sem, o_hi.at(i, w + 1))
                    dve.tensor_tensor(o_p[1][:, :, :].rearrange("p a t -> p (a t)"), bank["ot"][:, :],
                                      o_p[0][:, :, :].rearrange("p a t -> p (a t)").bitcast(F32), ALU.subtract)\
                        .then_inc(read["ot"].sem, 1)

                def add_attention(w):
                    src, back = wait_full(("wo", w))
                    stored = f_stored[w // UNIT]
                    dve.wait_ge(stored.sem, stored.at(i, 1) if w // UNIT == NU - 1 else stored.at(i, 0))
                    dve.tensor_tensor(fr[:, w, :], src[:, 0:C], fl[:, w, :], ALU.add).then_inc(back, 1)

                def moments(u):
                    w = UNIT * (u % NU)
                    _, n, _ = FILL_AT[("wo", w + UNIT - 1)]
                    count = lambda signal, n: signal.before(i, n) if u < 0 else signal.at(i, n)
                    dve.wait_ge(read["t"].sem, count(read["t"], n + 1))
                    dve.wait_ge(shifted.sem, count(shifted, min(2 * (w + UNIT), 2 * NWIN - 1)))
                    for t in range(UNIT):
                        dve.bn_stats(stats[:, t, 0, :], fr[:, w + t, 0:P])
                        ins = dve.bn_stats(stats[:, t, 1, :], hs[:, w + t, :])
                    step(ins)
                    dve.memset(var_tmp[:, 0:1], 0.0)
                    for t in range(UNIT):
                        ins = dve.bn_aggr(aggr[:, t, :], stats[:, t, :, :].rearrange("p a s -> p (a s)"))
                    step(ins)
                    step(dve.tensor_scalar(var[:, :], aggr[:, :, 1], LN_EPS, None, ALU.add))
                    seed_rsqrt(dve, dve_steps, rstd[:, :], var[:, :])
                    step(newton_rsqrt(dve, dve_steps, rstd[:, :], var[:, :], var_tmp[:, :]))

                def norm(u):
                    w = UNIT * (u % NU)
                    for _ in range(2):
                        step(newton_rsqrt(dve, dve_steps, rstd[:, :], var[:, :], var_tmp[:, :]))
                    for t in range(UNIT):
                        for src, cols in ((fr[:, w + t, 0:P], slice(0, P)), (hs[:, w + t, :], slice(P, C))):
                            ins = dve.tensor_scalar(hn[:, t, cols], src, aggr[:, t, 0:1], rstd[:, t:t + 1],
                                                    ALU.subtract, ALU.mult)
                    ins.then_inc(normed.sem, 1)

                def piece_of_mlp(piece, u, m):
                    if piece == "moments":
                        moments(u)
                    elif piece == "norm":
                        norm(u)
                    elif piece == "hT":
                        src, back = wait_full((piece, u, m))
                        for c in range(CK):
                            dve.tensor_scalar(h_scaled[:, c, :], src[:, c * UT:(c + 1) * UT], ln_g[:, c:c + 1],
                                              ln_b[:, c:c + 1], ALU.mult, ALU.add).then_inc(h_ready.sem, 1)
                        dve.wait_ge(h_ready.sem, h_ready.at(i, 2 * (u + 2)))
                        dve.sem_inc(back, 1)
                    elif piece == "product":
                        for m in range(HK):
                            dve.wait_ge(gelu_done.sem, gelu_done.at(i, HK * (u + 1) + m + 1))
                            ins = dve.scalar_tensor_tensor(out=ag[:, m, 0, :], in0=ag[:, m, 0, :],
                                                           scalar=b1_c[:, 0, m:m + 1], in1=ag[:, m, 1, :],
                                                           op0=ALU.add, op1=ALU.mult)
                            if m % (HK // 2) == HK // 2 - 1:
                                ins.then_inc(multiplied.sem, 1)
                    elif piece == "w2":
                        src, back = wait_full((piece, u, m))
                        dve.wait_ge(b2_added.sem, b2_added.at(i, u + 2))
                        rows = fr[:, blocks_of(u), :].rearrange("p t c -> p (t c)")
                        dve.tensor_tensor(rows, src[:, :], rows, ALU.add).then_inc(back, 1)

                def late_pieces(pp):
                    for x in pieces_at(pp, closing):
                        if x[0] in ("w2", "moments", "norm", "hT"):
                            piece_of_mlp(*x)

                for pp in range(FIRST, STEPS):
                    if not closing:
                        if pp in (FIRST, F_LATER):
                            split_f(int(pp == F_LATER))
                        if 0 <= pp - 1 < NPP:
                            shares(pp - 1)
                        if 0 <= pp < NPP:
                            row_tops(pp)
                    if pp < 0:
                        late_pieces(pp)
                    if not closing:
                        if pp % PAIRS == 0 and (pp + 4) // PAIRS < NWIN:
                            rotation_products((pp + 4) // PAIRS)
                        if pp % PAIRS == 1 and (pp + 3) // PAIRS < NWIN:
                            sum_squares((pp + 3) // PAIRS)
                            inverse_norms_begun((pp + 3) // PAIRS)
                        if pp % PAIRS == 2 and 0 <= (pp + 2) // PAIRS < NWIN:
                            inverse_norms((pp + 2) // PAIRS)
                    for x in pieces_at(pp, closing):
                        if x[0] == "product":
                            piece_of_mlp(*x)
                    if not closing:
                        if 0 <= pp - TURN_LAG < NPP and pp % 4 == 3:
                            take_turned(pp - TURN_LAG)
                        if 0 <= pp - MEET_LAG < NPP and (pp - MEET_LAG) % PAIRS == PAIRS - 1:
                            values_lo((pp - MEET_LAG) // PAIRS)
                        if 0 <= pp - OUT_LAG < NPP and (pp - OUT_LAG) % PAIRS == PAIRS - 1:
                            add_attention((pp - OUT_LAG) // PAIRS)
                    if pp >= 0:
                        late_pieces(pp)
                if not closing:
                    dve_steps.end()

            loop(dve, body)



_INS = (["L0_attn_x", "L0_c", "L0_wmod"] + ["L0_attn_W" + n for n in "qkvp"] + ["L0_attn_b" + n for n in "qkvp"]
        + ["L0_ffn_" + n for n in ("wqkv", "q_scale", "k_scale", "wo", "ln_g", "ln_b", "w1", "b1", "w2", "b2")])
DEPTH = 2


def stage(nc, program, *args):
    with ExitStack() as ctx:
        sems = Semaphores(nc, ctx)
        program(nc, sems, *args)
        clear(nc, sems.all)


def build(nc, ins, tables, out, turns=B):
    scratch = lambda name, shape, dt=F32: nc.dram_tensor(name, shape, dt, kind="Internal").ap()
    mod = scratch("mod_rows", (B, NMOD, C))
    x1 = scratch("x1_rows", (B, T, C))
    f = [scratch(f"f_rows{n}", (B, T, C)) for n in range(DEPTH)]
    parts = [scratch(f"parts_{n}", (3, C, T), BF16) for n in "qk"]
    maxima = scratch("maxima", (G1, 3, 4 * T), BF16)
    stage(nc, modulation_stage, ins["L0_c"], ins["L0_wmod"], mod)
    stage(nc, attention_stage, ins["L0_attn_x"], [ins["L0_attn_W" + n] for n in "qkvp"],
                    [ins["L0_attn_b" + n] for n in "qkvp"], mod, x1, f[0], parts, maxima, turns)
    for layer in range(DEPTH):
        w = {n: ins["L0_ffn_" + n][layer] for n in ("wqkv", "q_scale", "k_scale", "wo", "ln_g", "ln_b", "w1", "b1",
                                                    "w2", "b2")}
        final = layer == DEPTH - 1
        stage(nc, layer_stage, f"b{layer}", f[layer], out if final else f[layer + 1], tables, w["wqkv"], w["q_scale"],
                    w["k_scale"], w["wo"], w["ln_g"], w["ln_b"], w["w1"], w["b1"], w["w2"], w["b2"], mod, x1, turns,
                    final)


def kernel(**inputs):
    import concourse.bacc as _bacc
    from concourse.bass_utils import run_bass_kernel_spmd as _run

    nc = _bacc.Bacc("TRN2", target_bir_lowering=False, num_devices=1)
    arrays, ins = {}, {}
    for name in _INS:
        arrays[f"in_{name}"] = np.ascontiguousarray(inputs[name])
        ins[name] = nc.dram_tensor(f"in_{name}", arrays[f"in_{name}"].shape, F32, kind="ExternalInput").ap()
    arrays["rotary_tables"] = rotary_tables()
    tables = nc.dram_tensor("rotary_tables", (4, T, D2), F32, kind="ExternalInput").ap()
    out = nc.dram_tensor("out_0", (B, T, C), F32, kind="ExternalOutput").ap()
    build(nc, ins, tables, out)
    r = _run(nc, [arrays], core_ids=[0])
    return r.results[0]["out_0"]
```
